# Optimizing a Trainium2 kernel written in Bass

```python
import numpy as np
import jax
import jax.numpy as jnp

def _softmax(x, axis=-1):
    return jax.nn.softmax(x, axis=axis)

def _gelu(x):
    return jax.nn.gelu(x, approximate=True)

def _silu(x):
    return jax.nn.silu(x)

def _sigmoid(x):
    return jax.nn.sigmoid(x)

def _layernorm(x, axis=-1, eps=1e-05):
    m = jnp.mean(x, axis=axis, keepdims=True)
    v = jnp.var(x, axis=axis, keepdims=True)
    return (x - m) / jnp.sqrt(v + eps)

def _scatter_add(tgt, idx, src, axis=0):
    return tgt.at[idx].add(src)

def _segment_sum(src, seg, n):
    return jax.ops.segment_sum(src, seg, n)
kernel_name = 'mk_prb_d2_jaxref_r8_fe89d1'

def setup_inputs(seed: int=0):
    np.random.seed(seed)
    _w = jnp.asarray

    def _L0_attn_setup():
        import jax, jax.numpy as jnp
        import numpy as np
        import math
        B, S, HID, H = (2, 256, 128, 16)
        D = HID // H

        def _get_slopes(n):
            start = 2 ** (-2 ** (-(math.log2(n) - 3)))
            return np.array([start * 2 ** (-i) for i in range(n)], dtype=np.float32)
        key = jax.random.key(seed)
        ks = jax.random.split(key, 9)
        sc = 1.0 / math.sqrt(HID)
        return {'x': jax.random.normal(ks[0], (B, S, HID), dtype=jnp.float32), 'Wq': jax.random.normal(ks[1], (HID, HID), dtype=jnp.float32) * sc, 'bq': jnp.zeros((HID,), dtype=jnp.float32), 'Wk': jax.random.normal(ks[2], (HID, HID), dtype=jnp.float32) * sc, 'bk': jnp.zeros((HID,), dtype=jnp.float32), 'Wv': jax.random.normal(ks[3], (HID, HID), dtype=jnp.float32) * sc, 'bv': jnp.zeros((HID,), dtype=jnp.float32), 'Wo': jax.random.normal(ks[4], (HID, HID), dtype=jnp.float32) * sc, 'bo': jnp.zeros((HID,), dtype=jnp.float32), 'slopes': jnp.asarray(_get_slopes(H))}
    _L0_attn_in = _L0_attn_setup()

    def _L0_ffn_setup():
        import jax, jax.numpy as jnp
        import numpy as np
        TOP_K = 2

        def _swiglu_mlp(x, wgu, wd, inter):
            gu = x @ wgu
            a = jax.nn.silu(gu[:, :inter]) * gu[:, inter:]
            return a @ wd
        key = jax.random.key(seed)
        ks = jax.random.split(key, 6)
        H, I, E = (128, 352, 8)
        B, S = (2, 128)
        w = 0.02
        return {'x': jax.random.normal(ks[0], (B, S, H), jnp.float32), 'gate_w': jax.random.normal(ks[1], (H, E), jnp.float32) * w, 'base_wgu': jax.random.normal(ks[2], (H, 2 * I), jnp.float32) * w, 'base_wd': jax.random.normal(ks[3], (I, H), jnp.float32) * w, 'exp_wgu': jax.random.normal(ks[4], (E, H, 2 * I), jnp.float32) * w, 'exp_wd': jax.random.normal(ks[5], (E, I, H), jnp.float32) * w}
    _L0_ffn_in = _L0_ffn_setup()

    def _L1_attn_setup():
        import jax, jax.numpy as jnp
        import numpy as np
        import math
        NUM_HEADS = 16

        def _alibi_bias(L, num_heads):
            slopes = jnp.power(2.0, jnp.linspace(-4.0, -0.3, num_heads))
            pos = jnp.arange(L, dtype=jnp.float32)
            return -(slopes[:, None] * pos[None, :])
        key = jax.random.key(seed)
        ks = jax.random.split(key, 9)
        B, L, D = (2, 256, 128)
        s = 0.02
        return {'x': jax.random.normal(ks[0], (B, L, D), dtype=jnp.float32), 'Wq': jax.random.normal(ks[1], (D, D), dtype=jnp.float32) * s, 'bq': jax.random.normal(ks[2], (D,), dtype=jnp.float32) * s, 'Wk': jax.random.normal(ks[3], (D, D), dtype=jnp.float32) * s, 'bk': jax.random.normal(ks[4], (D,), dtype=jnp.float32) * s, 'Wv': jax.random.normal(ks[5], (D, D), dtype=jnp.float32) * s, 'bv': jax.random.normal(ks[6], (D,), dtype=jnp.float32) * s, 'Wo': jax.random.normal(ks[7], (D, D), dtype=jnp.float32) * s, 'bo': jax.random.normal(ks[8], (D,), dtype=jnp.float32) * s}
    _L1_attn_in = _L1_attn_setup()

    def _L1_ffn_setup():
        import jax, jax.numpy as jnp
        import numpy as np
        B, S, K, N = (8, 1024, 128, 128)
        key = jax.random.key(seed)
        k1, k2, k3, k4 = jax.random.split(key, 4)
        x = jax.random.normal(k1, (B, S, K), dtype=jnp.float32)
        CB = jnp.clip(jnp.round(jax.random.normal(k2, (N, K), dtype=jnp.float32) * 42.0), -127.0, 127.0)
        SCB = jax.random.uniform(k3, (N,), dtype=jnp.float32, minval=0.5, maxval=2.0)
        bias = jax.random.normal(k4, (N,), dtype=jnp.float32) * 0.02
        return {'x': x, 'CB': CB, 'SCB': SCB, 'bias': bias}
    _L1_ffn_in = _L1_ffn_setup()
    _d = {'L0_attn_x': _L0_attn_in['x'], 'L0_attn_Wq': _L0_attn_in['Wq'], 'L0_attn_bq': _L0_attn_in['bq'], 'L0_attn_Wk': _L0_attn_in['Wk'], 'L0_attn_bk': _L0_attn_in['bk'], 'L0_attn_Wv': _L0_attn_in['Wv'], 'L0_attn_bv': _L0_attn_in['bv'], 'L0_attn_Wo': _L0_attn_in['Wo'], 'L0_attn_bo': _L0_attn_in['bo'], 'L0_attn_slopes': _L0_attn_in['slopes'], 'L0_ffn_gate_w': _L0_ffn_in['gate_w'], 'L0_ffn_base_wgu': _L0_ffn_in['base_wgu'], 'L0_ffn_base_wd': _L0_ffn_in['base_wd'], 'L0_ffn_exp_wgu': _L0_ffn_in['exp_wgu'], 'L0_ffn_exp_wd': _L0_ffn_in['exp_wd'], 'L1_attn_Wq': _L1_attn_in['Wq'], 'L1_attn_bq': _L1_attn_in['bq'], 'L1_attn_Wk': _L1_attn_in['Wk'], 'L1_attn_bk': _L1_attn_in['bk'], 'L1_attn_Wv': _L1_attn_in['Wv'], 'L1_attn_bv': _L1_attn_in['bv'], 'L1_attn_Wo': _L1_attn_in['Wo'], 'L1_attn_bo': _L1_attn_in['bo'], 'L1_ffn_CB': _L1_ffn_in['CB'], 'L1_ffn_SCB': _L1_ffn_in['SCB'], 'L1_ffn_bias': _L1_ffn_in['bias']}
    _x0 = _d['L0_attn_x']
    _d['L0_attn_x'] = jax.random.normal(jax.random.fold_in(jax.random.key(seed), 1), (32, 256, 128), dtype=_x0.dtype)
    del _x0
    return _d

def reference(L0_attn_x, L0_attn_Wq, L0_attn_bq, L0_attn_Wk, L0_attn_bk, L0_attn_Wv, L0_attn_bv, L0_attn_Wo, L0_attn_bo, L0_attn_slopes, L0_ffn_gate_w, L0_ffn_base_wgu, L0_ffn_base_wd, L0_ffn_exp_wgu, L0_ffn_exp_wd, L1_attn_Wq, L1_attn_bq, L1_attn_Wk, L1_attn_bk, L1_attn_Wv, L1_attn_bv, L1_attn_Wo, L1_attn_bo, L1_ffn_CB, L1_ffn_SCB, L1_ffn_bias):

    def _L0_attn_ref(x, Wq, bq, Wk, bk, Wv, bv, Wo, bo, slopes):
        import jax, jax.numpy as jnp
        import numpy as np
        import math
        B, S, HID, H = (2, 256, 128, 16)
        D = HID // H

        def _get_slopes(n):
            start = 2 ** (-2 ** (-(math.log2(n) - 3)))
            return np.array([start * 2 ** (-i) for i in range(n)], dtype=np.float32)
        b, s, hid = x.shape
        h = slopes.shape[0]
        d = hid // h
        q = (x @ Wq.T + bq).reshape(b, s, h, d).transpose(0, 2, 1, 3)
        k = (x @ Wk.T + bk).reshape(b, s, h, d).transpose(0, 2, 1, 3)
        v = (x @ Wv.T + bv).reshape(b, s, h, d).transpose(0, 2, 1, 3)
        scores = jnp.einsum('bhqd,bhkd->bhqk', q, k) / jnp.sqrt(jnp.float32(d))
        pos = jnp.arange(s)
        dist = (pos[None, :] - pos[:, None]).astype(x.dtype)
        scores = scores + slopes[None, :, None, None] * dist[None, None]
        attn = jax.nn.softmax(scores, axis=-1)
        ctx = jnp.einsum('bhqk,bhkd->bhqd', attn, v)
        ctx = ctx.transpose(0, 2, 1, 3).reshape(b, s, hid)
        return ctx @ Wo.T + bo

    def _L0_ffn_ref(x, gate_w, base_wgu, base_wd, exp_wgu, exp_wd):
        import jax, jax.numpy as jnp
        import numpy as np
        TOP_K = 2

        def _swiglu_mlp(x, wgu, wd, inter):
            gu = x @ wgu
            a = jax.nn.silu(gu[:, :inter]) * gu[:, inter:]
            return a @ wd
        orig_shape = x.shape
        H = orig_shape[-1]
        I = base_wd.shape[0]
        E = gate_w.shape[1]
        xt = x.reshape(-1, H)
        T = xt.shape[0]
        base_y = _swiglu_mlp(xt, base_wgu, base_wd, I)
        logits = xt @ gate_w
        probs = jax.nn.softmax(logits.astype(jnp.float32), axis=-1)
        topw, topi = jax.lax.top_k(probs, TOP_K)
        topw = topw / jnp.sum(topw, axis=-1, keepdims=True)
        topw = topw.astype(x.dtype)
        cw = jnp.zeros((T, E), x.dtype).at[jnp.arange(T)[:, None], topi].add(topw)
        out = base_y
        for e in range(E):
            ye = _swiglu_mlp(xt, exp_wgu[e], exp_wd[e], I)
            out = out + cw[:, e:e + 1] * ye
        return out.reshape(orig_shape)

    def _L1_attn_ref(x, Wq, bq, Wk, bk, Wv, bv, Wo, bo):
        import jax, jax.numpy as jnp
        import numpy as np
        import math
        NUM_HEADS = 16

        def _alibi_bias(L, num_heads):
            slopes = jnp.power(2.0, jnp.linspace(-4.0, -0.3, num_heads))
            pos = jnp.arange(L, dtype=jnp.float32)
            return -(slopes[:, None] * pos[None, :])
        B, L, D = x.shape
        H = NUM_HEADS
        hd = D // H
        scale = math.sqrt(hd)

        def proj(W, b):
            return (jnp.einsum('bld,ed->ble', x, W) + b).reshape(B, L, H, hd)
        q = proj(Wq, bq)
        k = proj(Wk, bk)
        v = proj(Wv, bv)
        scores = jnp.einsum('bqhd,bkhd->bhqk', q, k) / scale
        bias = _alibi_bias(L, H)
        scores = scores + bias[None, :, None, :]
        attn = jax.nn.softmax(scores, axis=-1)
        out = jnp.einsum('bhqk,bkhd->bqhd', attn, v).reshape(B, L, D)
        return jnp.einsum('bld,ed->ble', out, Wo) + bo

    def _L1_ffn_ref(x, CB, SCB, bias):
        import jax, jax.numpy as jnp
        import numpy as np
        B, S, K, N = (8, 1024, 128, 128)
        out = jnp.einsum('bsk,nk->bsn', x, CB)
        out = out * (SCB * (1.0 / 127.0)) + bias
        return out
    x = L0_attn_x
    xn = _layernorm(x, axis=-1)
    x = x + _L0_attn_ref(xn, L0_attn_Wq, L0_attn_bq, L0_attn_Wk, L0_attn_bk, L0_attn_Wv, L0_attn_bv, L0_attn_Wo, L0_attn_bo, L0_attn_slopes) + _L0_ffn_ref(xn, L0_ffn_gate_w, L0_ffn_base_wgu, L0_ffn_base_wd, L0_ffn_exp_wgu, L0_ffn_exp_wd)
    xn = _layernorm(x, axis=-1)
    x = x + _L1_attn_ref(xn, L1_attn_Wq, L1_attn_bq, L1_attn_Wk, L1_attn_bk, L1_attn_Wv, L1_attn_bv, L1_attn_Wo, L1_attn_bo) + _L1_ffn_ref(xn, L1_ffn_CB, L1_ffn_SCB, L1_ffn_bias)
    return x

_drawn_inputs = setup_inputs


def setup_inputs(seed=0):
    import zlib

    import numpy as np

    out = dict(_drawn_inputs(seed))
    spreads = {'L0_attn_bq': (0.0, 2.0),
     'L0_attn_bk': (0.0, 2.0),
     'L0_attn_bv': (0.0, 0.45),
     'L0_attn_bo': (0.0, 0.399)}
    factors = {'L0_ffn_gate_w': 8.0,
     'L0_ffn_base_wgu': 6.1,
     'L0_ffn_base_wd': 6.134,
     'L0_ffn_exp_wgu': 8.0,
     'L0_ffn_exp_wd': 8.0,
     'L1_attn_Wq': 8.0,
     'L1_attn_bq': 8.0,
     'L1_attn_Wk': 8.0,
     'L1_attn_bk': 64.0,
     'L1_attn_Wv': 8.0,
     'L1_attn_bv': 8.0,
     'L1_attn_Wo': 8.0,
     'L1_attn_bo': 22.135,
     'L1_ffn_bias': 22.637}
    for name, (base, spread) in spreads.items():
        noise = np.random.default_rng([zlib.crc32(name.encode()), seed]).standard_normal(out[name].shape)
        drawn = base * np.exp(spread * noise) if base else spread * noise
        out[name] = jnp.asarray(drawn.astype(out[name].dtype))
    for name, factor in factors.items():
        out[name] = (out[name] * factor).astype(out[name].dtype)
    return out
```

```python
import numpy as np
from contextlib import ExitStack

import concourse.bass as bass
from concourse import mybir

BATCHES, SEQ, HID = 32, 256, 128
HEADS = 16
HEAD_DIM = HID // HEADS
INTER = 352
EXPERTS = 8
MLPS = EXPERTS + 1
QT = SEQ // 128
FT = -(-INTER // 128)
F_ROWS = [min(128, INTER - 128 * f) for f in range(FT)]
UNITS = MLPS * FT
TURNS = BATCHES + 1
EPS = 1e-5

X_SCALE = 16.0
W_SCALE = 64.0
A_SCALE = 16.0
QK_SCALE = 32.0
SIGMA = QK_SCALE * QK_SCALE
GU_SCALE = X_SCALE * W_SCALE
Y_SCALE = A_SCALE * W_SCALE

STRIP = 64
PARTS = 8
MAX_ROW = PARTS * (HEAD_DIM - 1) + 3


def order_of_stages():
    unit = iter(range(UNITS + 8))
    mlp = lambda: ("mlp", 0, next(unit))
    s = [("start", 0, 0), ("load", 0, 0), mlp(), ("norm", 1, 0), mlp(), ("max", 0, 0), mlp(), ("max", 0, 1),
         ("xT", 1, 0), mlp(), ("max", 0, 2), ("qk", 1, 0), mlp(), ("max", 0, 3), ("split_qk", 1, 0), ("v", 1, 0),
         mlp(), ("max", 0, 4), mlp(), ("max", 0, 5), mlp(), ("max", 0, 6), mlp(), ("max", 0, 7), mlp(),
         ("maxT", 0, 0), mlp(), mlp(), mlp()]
    for n in range(8):
        s += [("exp", 0, n), ("max", 1, n)][::-1 if n % 2 else 1]
        if n % 2 and n >= 3:
            s += [("pv", 0, (n - 3) // 2), mlp()]
        if n % 2 == 0 and n >= 4:
            s += [("norm_ctx", 0, (n - 4) // 2)]
    s += [("pv", 0, 3), ("norm_ctx", 0, 2), mlp(), ("maxT", 1, 0), mlp(), ("norm_ctx", 0, 3), mlp(), ("ctxT", 0, 0), mlp()]
    extra = {0: [("norm", 0, 0)], 1: [("xT", 0, 0)], 2: [("qk", 0, 0)], 3: [("v", 0, 0), ("split_qk", 0, 0)], 4: [("router", 0, 0)]}
    for n in range(8):
        s += [("exp", 1, n), mlp()]
        if n % 2 and n >= 3:
            s += [("pv", 1, (n - 3) // 2)]
        if n % 2 == 0 and n >= 4:
            s += [("norm_ctx", 1, (n - 4) // 2)]
        s += extra.get(n, [])
    s += [("pv", 1, 3), ("norm_ctx", 1, 2), ("cw", 0, 0), mlp(), ("split_x", 0, 0), ("norm_ctx", 1, 3), mlp(), ("ctxT", 1, 0)]
    s += [mlp(), ("out", 1, 0)]
    n = s.count
    done = sum(1 for k, _, _ in s if k == "mlp")
    s += [mlp() for _ in range(UNITS + DRAIN - done)]
    return s + [("out", 0, 0)]


DRAIN = 5
STAGES = order_of_stages()
PREPARE = [("norm", 0, 0), ("xT", 0, 0), ("qk", 0, 0), ("split_qk", 0, 0), ("v", 0, 0), ("router", 0, 0), ("cw", 0, 0), ("split_x", 0, 0)]
MISC = ("xT", "qk", "v", "router", "maxT", "pv", "norm_ctx", "ctxT", "out")


class Signal:

    def __init__(self, sem, per, before=0):
        self.sem, self.per, self.before = sem, per, before

    def at(self, turn, k):
        return turn * self.per + (self.before + k)


def places(stages, kinds):
    found = [s for s in stages if s[0] in kinds]
    return {s: n + 1 for n, s in enumerate(found)}


def build(nc, x, w_gu, w_down, w_sq, cb, gate, b_col, b_row, slopes, pos, sigma_row, ident_in, iota_in, out):
    f32, f16, u32 = mybir.dt.float32, mybir.dt.float16, mybir.dt.uint32
    ALU, ACT, AX = mybir.AluOpType, mybir.ActivationFunctionType, mybir.AxisListType
    misc_at, misc_first = places(STAGES, MISC), places(PREPARE, MISC)
    score_at = places(STAGES, ("max", "exp"))
    group_at = {("exp", l, n): 4 * l + n // 2 for l in (0, 1) for n in range(8)}

    with ExitStack() as ctx:
        def sb(name, shape, dt=f32):
            return ctx.enter_context(nc.sbuf_tensor(name, shape, dt))

        def sem(name):
            return ctx.enter_context(nc.semaphore(name))

        wgu32 = sb("wgu32", [128, MLPS * 2 * INTER])
        wd32 = sb("wd32", [128, MLPS * FT * 128])
        wgu = sb("wgu", [128, 2, MLPS, 2, INTER], f16)
        wd = sb("wd", [128, 2, MLPS, FT, 128], f16)
        wsq = sb("wsq", [128, 8, 128])
        cbs = sb("cbs", [128, 128])
        gates = sb("gates", [128, EXPERTS])
        bcol = sb("bcol", [128, 4])
        bcols = sb("bcols", [128, 4])
        brow = sb("brow", [128, 6, QT, 128])
        ident = sb("ident", [128, 128])
        iota = sb("iota", [128, EXPERTS])
        slope32, slope_rest = sb("slope32", [2, HEADS]), sb("slope_rest", [2, HEADS])
        slope_part = sb("slope_part", [2, 3, HEADS], f16)
        x_in = sb("x_in", [128, QT, HID])
        acc = sb("acc", [128, QT, HID])
        x_mid = sb("x_mid", [128, QT, HID])
        res1 = sb("res1", [128, QT, HID])
        y_out = sb("y_out", [128, QT, HID])
        x16 = sb("x16", [128, 2, SEQ], f16)
        both = lambda name, shape, dt=f32: [sb(f"{name}{l}", shape, dt) for l in (0, 1)]
        stats, mv, rstd = both("stats", [128, QT, 6]), both("mv", [128, QT, 2]), both("rstd", [128, QT])
        var = both("var", [128, QT])
        minus_half = sb("minus_half", [128, QT])
        xn, xs = both("xn", [128, QT, HID]), both("xs", [128, SEQ])
        qk32, qk16 = both("qk32", [128, 2, SEQ]), both("qk16", [128, 2, 2, SEQ], f16)
        QS, KS = both("QS", [128, HEADS // 2, SEQ], f16), both("KS", [128, HEADS // 2, SEQ], f16)
        V = both("V", [128, QT, HEADS, 32])
        row_max, max_t = both("row_max", [128, QT, HEADS]), both("max_t", [HEADS, SEQ], f16)
        ctx_n, ctx_t = both("ctx_n", [128, QT, HID]), both("ctx_t", [128, SEQ])
        prob = sb("prob", [128, 2, QT, 2, 2, SEQ])
        slope16 = sb("slope16", [2, 3, HEADS * SEQ], f16)
        pv_sb = sb("pv_sb", [128, 2, SEQ])
        rden = sb("rden", [128, QT, 4])
        tanh_sb, gated = sb("tanh_sb", [128, 2, SEQ]), sb("gated", [128, 2, SEQ])
        a32 = sb("a32", [128, 4, SEQ])
        a16 = sb("a16", [128, 4, 2, SEQ], f16)
        logit = sb("logit", [128, QT, EXPERTS])
        top = sb("top", [128, QT, 8])
        topi = sb("topi", [128, QT, 8], u32)
        topf = sb("topf", [128, QT, 2])
        gap, e2, den = sb("gap", [128, QT]), sb("e2", [128, QT]), sb("den", [128, QT])
        w12 = sb("w12", [128, QT, 2])
        pick = sb("pick", [128, 2, QT, EXPERTS])
        cw = sb("cw", [128, QT, EXPERTS])

        ps_score = [ctx.enter_context(nc.psum_tensor(f"ps_score{n}", [128, 2, 2, SEQ], f32)) for n in (0, 1)]
        ps_gu = [ctx.enter_context(nc.psum_tensor(f"ps_gu{n}", [128, 2, SEQ], f32)) for n in (0, 1)]
        ps_y = ctx.enter_context(nc.psum_tensor("ps_y", [128, 512], f32))
        ps_misc = ctx.enter_context(nc.psum_tensor("ps_misc", [128, 512], f32))

        scratch = [nc.dram_tensor(f"scratch{l}", [2, 2, 128, SEQ], f16, kind="Internal").ap() for l in (0, 1)]

        P0 = len(misc_first)
        weights_in = sem("weights_in")
        consts_in = sem("consts_in")
        slopes_split = sem("slopes_split")
        cleared = sem("cleared")
        weights_split = sem("weights_split")
        small_ready = sem("small_ready")
        misc_full = Signal(sem("misc_full"), len(misc_at), P0)
        misc_out = Signal(sem("misc_out"), len(misc_at), P0)
        score_full = Signal(sem("score_full"), len(score_at))
        score_used = [Signal(sem(f"score_used{n}"), len(score_at) // 2, 1) for n in (0, 1)]
        gu_full = Signal(sem("gu_full"), UNITS)
        tanh_done = Signal(sem("tanh_done"), UNITS)
        gated_done = Signal(sem("gated_done"), UNITS)
        a_done = Signal(sem("a_done"), UNITS, 2)
        hi_done = Signal(sem("hi_done"), UNITS)
        lo_done = Signal(sem("lo_done"), UNITS)
        y_full = Signal(sem("y_full"), MLPS)
        y_used = Signal(sem("y_used"), MLPS, 1)
        started = Signal(sem("started"), 1)
        x_loaded = Signal(sem("x_loaded"), 16, 16)
        normed = [Signal(sem(f"normed{l}"), 1, 1 - l) for l in (0, 1)]
        x_split = Signal(sem("x_split"), 1, 1)
        qk_split = [Signal(sem(f"qk_split{l}"), 1, 1 - l) for l in (0, 1)]
        qk_written = [Signal(sem(f"qk_written{l}"), 16, 16 * (1 - l)) for l in (0, 1)]
        qk_read = [Signal(sem(f"qk_read{l}"), 96, 96 * (1 - l)) for l in (0, 1)]
        max_read = [Signal(sem(f"max_read{l}"), 32) for l in (0, 1)]
        var_done = [Signal(sem(f"var_done{l}"), 1, 1 - l) for l in (0, 1)]
        rstd_done = [Signal(sem(f"rstd_done{l}"), 1, 1 - l) for l in (0, 1)]
        gap_ready = Signal(sem("gap_ready"), 1, 1)
        e2_ready = Signal(sem("e2_ready"), 1, 1)
        stored = Signal(sem("stored"), 16, 1)
        dve_link = Signal(sem("dve_link"), DVE_LINKS, DVE_LINKS_FIRST)

        def misc_k(stage, first):
            return misc_first[stage] - P0 if first else misc_at[stage]

        CONSTS = 16 * 8

        block = ctx.enter_context(nc.Block())

        @block.sync
        def _(sp):
            for dst, src in ((wsq[:, :, :], w_sq), (gates[:, :], gate), (bcol[:, :], b_col), (ident[:, :], ident_in),
                             (iota[:, :], iota_in), (brow[:, :, :, :], b_row), (cbs[:, :], cb), (slope32[:, :], slopes)):
                sp.dma_start(dst, src).then_inc(consts_in, 16)
            sp.dma_start(x_in[:, :, :], x[0]).then_inc(x_loaded.sem, 16)
            sp.dma_start(wgu32[:, :], w_gu).then_inc(weights_in, 16)
            sp.dma_start(wd32[:, :], w_down).then_inc(weights_in, 16)
            sp.wait_ge(cleared, 1)
            for l in (0, 1):
                for j in (0, 1):
                    for d in range(3):
                        row = STRIP * j + PARTS * d + 3
                        sp.dma_start(KS[l][row:row + 1, :, :], pos).then_inc(small_ready, 16)
                    row = STRIP * j + MAX_ROW
                    sp.dma_start(KS[l][row:row + 1, :, :], sigma_row).then_inc(small_ready, 16)
            sp.wait_ge(slopes_split, 1)
            for l in (0, 1):
                for j in (0, 1):
                    for d in range(3):
                        row = STRIP * j + PARTS * d + 3
                        src = slope16[l:l + 1, d, :].rearrange("p (g j t) -> p j g t", j=2, t=SEQ)[:, j]
                        sp.dma_start(QS[l][row:row + 1, :, :], src).then_inc(small_ready, 16)

            def stage(kind, l, n, i, first):
                if kind == "load":
                    sp.wait_ge(started.sem, started.at(i, 1))
                    sp.dma_start(x_in[:, :, :], x[i + 1]).then_inc(x_loaded.sem, 16)
                elif kind == "split_qk":
                    sp.wait_ge(qk_split[l].sem, qk_split[l].at(i, 0 if first else 1))
                    if l == 0 and not first:
                        sp.wait_ge(score_full.sem, score_full.at(i, score_at[("exp", 0, 7)]))
                    sp.dma_start(scratch[l].rearrange("a s p t -> p a s t"), qk16[l][:, :, :, :]).then_inc(qk_written[l].sem, 16)
                    sp.wait_ge(qk_written[l].sem, qk_written[l].at(i, 0 if first else 16))
                    for side, strips, halves in ((0, QS[l], (0, 0, 1)), (1, KS[l], (0, 1, 0))):
                        for r, half in enumerate(halves):
                            sp.dma_start(strips[r:128:PARTS, :, :],
                                         scratch[l][half, side].rearrange("(g p) t -> p g t", p=16)).then_inc(qk_read[l].sem, 16)
                elif kind == "maxT":
                    sp.wait_ge(misc_out.sem, misc_out.at(i, misc_k(("maxT", l, 0), False)))
                    for j in (0, 1):
                        row = STRIP * j + MAX_ROW
                        sp.dma_start(QS[l][row:row + 1, :, :], max_t[l][j:HEADS:2, :]).then_inc(max_read[l].sem, 16)
                elif kind == "out" and l == 1:
                    sp.wait_ge(misc_out.sem, misc_out.at(i, misc_k(("out", 1, 0), False)))
                    sp.dma_start(out[i], y_out[:, :, :]).then_inc(stored.sem, 16)

            for s in PREPARE:
                stage(*s, 0, True)
            with sp.Fori(0, TURNS) as i:
                for s in STAGES:
                    stage(*s, i, False)
            sp.wait_ge(stored.sem, stored.at(TURNS, 0))
            for l in (0, 1):
                sp.wait_ge(qk_written[l].sem, qk_written[l].at(TURNS, 0))

        @block.gpsimd
        def _(pool):
            for l in (0, 1):
                nc.gpsimd.memset(QS[l][:, :, :], 0.0)
                last = nc.gpsimd.memset(KS[l][:, :, :], 0.0)
            last.then_inc(cleared, 1)
            nc.gpsimd.memset(minus_half[:, :], -0.5).then_inc(cleared, 1)
            pool.wait_ge(cleared, 2)

            def low(n, i):
                rows = F_ROWS[n % FT]
                pool.wait_ge(hi_done.sem, hi_done.at(i, n + 1))
                nc.gpsimd.tensor_tensor(a16[:rows, n % 4, 1, :], a32[:rows, n % 4, :], a16[:rows, n % 4, 0, :],
                                        ALU.subtract).then_inc(lo_done.sem, 1)

            def inverse_root(l, i, first):
                pool.wait_ge(var_done[l].sem, var_done[l].at(i, 0 if first else 1))
                nc.gpsimd.tensor_tensor(rstd[l][:, :], var[l][:, :], minus_half[:, :], ALU.pow).then_inc(rstd_done[l].sem, 1)

            inverse_root(0, 0, True)
            with pool.Fori(0, TURNS) as i:
                for kind, l, n in STAGES:
                    if kind == "norm":
                        inverse_root(l, i, False)
                    if kind == "mlp" and 0 <= n - 3 < UNITS:
                        low(n - 3, i)

        @block.scalar
        def _(act):
            def stage(kind, l, n, i, first):
                if kind == "mlp":
                    if 0 <= n - 3 < UNITS:
                        u = n - 3
                        rows = F_ROWS[u % FT]
                        act.wait_ge(a_done.sem, a_done.at(i, u + 1))
                        nc.scalar.activation(a16[:rows, u % 4, 0, :], a32[:rows, u % 4, :], ACT.Copy).then_inc(hi_done.sem, 1)
                    if n < UNITS:
                        rows = F_ROWS[n % FT]
                        act.wait_ge(gu_full.sem, gu_full.at(i, n + 1))
                        if n >= 2:
                            act.wait_ge(gated_done.sem, gated_done.at(i, n - 1))
                        nc.scalar.activation(tanh_sb[:rows, n % 2, :], ps_gu[n % 2][:rows, 0, :], ACT.Tanh,
                                             scale=0.5 / GU_SCALE).then_inc(tanh_done.sem, 1)
                elif kind == "exp":
                    k = score_at[(kind, l, n)]
                    act.wait_ge(score_full.sem, score_full.at(i, k))
                    buf = group_at[(kind, l, n)] % 2
                    nc.scalar.activation(prob[:, buf, n % 2], ps_score[(k - 1) % 2][:, :, :, :], ACT.Exp,
                                         scale=1.0 / SIGMA).then_inc(score_used[(k - 1) % 2].sem, 1)
                elif kind in ("xT", "qk", "maxT", "pv", "ctxT"):
                    k = misc_k((kind, l, n), first)
                    act.wait_ge(misc_full.sem, misc_full.at(i, k))
                    if kind == "xT":
                        last = nc.scalar.activation(xs[l][:, :], ps_misc[:, 0:SEQ], ACT.Copy, scale=X_SCALE)
                    elif kind == "qk":
                        nc.scalar.activation(qk32[l][:, 0, :], ps_misc[:, 0:SEQ], ACT.Identity, bias=bcols[:, 2 * l:2 * l + 1],
                                             scale=QK_SCALE / X_SCALE / float(np.sqrt(HEAD_DIM)))
                        last = nc.scalar.activation(qk32[l][:, 1, :], ps_misc[:, SEQ:2 * SEQ], ACT.Identity,
                                                    bias=bcols[:, 2 * l + 1:2 * l + 2], scale=QK_SCALE / X_SCALE)
                    elif kind == "maxT":
                        last = nc.scalar.activation(max_t[l][:, :], ps_misc[0:HEADS, 0:SEQ], ACT.Copy, scale=-1.0 / SIGMA)
                    elif kind == "pv":
                        last = nc.scalar.activation(pv_sb[:, n % 2, :], ps_misc[:, 0:SEQ], ACT.Copy)
                    else:
                        last = nc.scalar.activation(ctx_t[l][:, :], ps_misc[:, 0:SEQ], ACT.Copy)
                    last.then_inc(misc_out.sem, 1)
                elif kind == "router":
                    act.wait_ge(gap_ready.sem, gap_ready.at(i, 0 if first else 1))
                    nc.scalar.activation(e2[:, :], gap[:, :], ACT.Exp).then_inc(e2_ready.sem, 1)

            act.wait_ge(weights_split, 1)
            for s in PREPARE:
                stage(*s, 0, True)
            with act.Fori(0, TURNS) as i:
                for s in STAGES:
                    stage(*s, i, False)

        @block.vector
        def _(dve):
            marks = [0]

            def link(ins, i, first, plain=False):
                marks[0] += 1
                ins.then_inc(dve_link.sem, 1)
                value = dve.to_reg(dve_link.at(i, marks[0] - (DVE_LINKS_FIRST if first else 0)))
                if plain:
                    dve.wait_ge(consts_in, CONSTS)
                dve.wait_ge(dve_link.sem, value)

            def stage(kind, l, n, i, first):
                if kind == "start":
                    dve.wait_ge(misc_out.sem, misc_out.at(i, 0))
                    nc.vector.tensor_copy(cw[:, :, :], pick[:, 0])
                    nc.vector.tensor_tensor(acc[:, :, :], x_in[:, :, :], brow[:, 1], ALU.add).then_inc(started.sem, 1)
                elif kind == "norm":
                    src = x_mid if l else x_in
                    if l == 0:
                        dve.wait_ge(x_loaded.sem, x_loaded.at(i, 0 if first else 16))
                    else:
                        dve.wait_ge(misc_out.sem, misc_out.at(i, 0))
                    for t in range(QT):
                        last = nc.vector.bn_stats(stats[l][:, t, :], src[:, t, :])
                    link(last, i, first, plain=True)
                    for t in range(QT):
                        last = nc.vector.bn_aggr(mv[l][:, t, :], stats[l][:, t, :])
                    link(last, i, first)
                    nc.vector.tensor_scalar(var[l][:, :], mv[l][:, :, 1], EPS, None, ALU.add).then_inc(var_done[l].sem, 1)
                    if l:
                        nc.vector.tensor_tensor(res1[:, :, :], x_mid[:, :, :], brow[:, 3], ALU.add)
                    dve.wait_ge(rstd_done[l].sem, rstd_done[l].at(i, 0 if first else 1))
                    for t in range(QT):
                        last = nc.vector.tensor_scalar(xn[l][:, t, :], src[:, t, :], mv[l][:, t, 0:1], rstd[l][:, t:t + 1],
                                                       ALU.subtract, ALU.mult)
                    last.then_inc(normed[l].sem, 1)
                elif kind == "max":
                    k = score_at[(kind, l, n)]
                    dve.wait_ge(score_full.sem, score_full.at(i, k))
                    a, t = n // 2, n % 2
                    dst = row_max[l][:, t, 4 * a:4 * a + 4].rearrange("p (g j) -> p j g", j=2)
                    nc.vector.tensor_reduce(dst, ps_score[(k - 1) % 2][:, :, :, :], axis=AX.X,
                                            op=ALU.max).then_inc(score_used[(k - 1) % 2].sem, 1)
                elif kind == "mlp":
                    done = n - 5
                    if 0 <= done < UNITS and done % FT == FT - 1:
                        m = done // FT
                        dve.wait_ge(y_full.sem, y_full.at(i, m + 1))
                        if m:
                            dve.wait_ge(y_used.sem, y_used.at(i, m))
                        else:
                            dve.wait_ge(started.sem, started.at(i, 1))
                        for t in range(QT):
                            by = 1.0 / Y_SCALE if m == 0 else cw[:, t, m - 1:m]
                            last = nc.vector.scalar_tensor_tensor(acc[:, t, :], ps_y[:, 128 * t:128 * t + 128], by, acc[:, t, :],
                                                                  op0=ALU.mult, op1=ALU.add)
                        last.then_inc(y_used.sem, 1)
                    if 0 <= n - 2 < UNITS:
                        u = n - 2
                        rows = F_ROWS[u % FT]
                        dve.wait_ge(gated_done.sem, gated_done.at(i, u + 1))
                        nc.vector.scalar_tensor_tensor(a32[:rows, u % 4, :], gated[:rows, u % 2, :], 0.5 * A_SCALE / GU_SCALE ** 2,
                                                       ps_gu[u % 2][:rows, 1, :], op0=ALU.mult, op1=ALU.mult).then_inc(a_done.sem, 1)
                    if 0 <= n - 1 < UNITS:
                        u = n - 1
                        rows = F_ROWS[u % FT]
                        dve.wait_ge(tanh_done.sem, tanh_done.at(i, u + 1))
                        nc.vector.scalar_tensor_tensor(gated[:rows, u % 2, :], tanh_sb[:rows, u % 2, :], 1.0,
                                                       ps_gu[u % 2][:rows, 0, :], op0=ALU.add, op1=ALU.mult).then_inc(gated_done.sem, 1)
                elif kind == "split_qk":
                    dve.wait_ge(misc_out.sem, misc_out.at(i, misc_k(("qk", l, 0), first)))
                    link(nc.vector.tensor_copy(qk16[l][:, 0], qk32[l][:, :, :]), i, first)
                    nc.vector.tensor_tensor(qk16[l][:, 1], qk32[l][:, :, :], qk16[l][:, 0], ALU.subtract).then_inc(qk_split[l].sem, 1)
                elif kind == "split_x":
                    if not first:
                        dve.wait_ge(gu_full.sem, gu_full.at(i, UNITS))
                    dve.wait_ge(misc_out.sem, misc_out.at(i, misc_k(("xT", 0, 0), first)))
                    link(nc.vector.tensor_copy(x16[:, 0, :], xs[0][:, :]), i, first)
                    nc.vector.tensor_tensor(x16[:, 1, :], xs[0][:, :], x16[:, 0, :], ALU.subtract).then_inc(x_split.sem, 1)
                elif kind == "v":
                    k = misc_k((kind, l, n), first)
                    dve.wait_ge(misc_full.sem, misc_full.at(i, k))
                    nc.vector.scalar_tensor_tensor(
                        V[l][:, :, :, 0:HEAD_DIM], ps_misc[:, 0:QT * HID].rearrange("p (t h d) -> p t h d", t=QT, d=HEAD_DIM),
                        1.0 / X_SCALE, brow[:, 2 * l].rearrange("p t (h d) -> p t h d", d=HEAD_DIM),
                        op0=ALU.mult, op1=ALU.add).then_inc(misc_out.sem, 1)
                elif kind == "router":
                    k = misc_k((kind, l, n), first)
                    dve.wait_ge(misc_full.sem, misc_full.at(i, k))
                    nc.vector.tensor_scalar(logit[:, :, :], ps_misc[:, 0:QT * EXPERTS].rearrange("p (t e) -> p t e", t=QT),
                                            1.0 / X_SCALE, None, ALU.mult).then_inc(misc_out.sem, 1)
                    dve.wait_ge(consts_in, CONSTS)
                    dve.wait_ge(misc_out.sem, misc_out.at(i, k))
                    for t in range(QT):
                        last = nc.vector.max(top[:, t, :], logit[:, t, :])
                    link(last, i, first)
                    nc.vector.tensor_tensor(gap[:, :], top[:, :, 1], top[:, :, 0], ALU.subtract).then_inc(gap_ready.sem, 1)
                    for t in range(QT):
                        last = nc.vector.max_index(topi[:, t, :], top[:, t, :], logit[:, t, :])
                    link(last, i, first)
                    nc.vector.tensor_copy(topf[:, :, :], topi[:, :, 0:2])
                elif kind == "cw":
                    dve.wait_ge(e2_ready.sem, e2_ready.at(i, 0 if first else 1))
                    link(nc.vector.tensor_scalar(den[:, :], e2[:, :], 1.0, None, ALU.add), i, first)
                    link(nc.vector.reciprocal(w12[:, :, 0], den[:, :]), i, first)
                    link(nc.vector.scalar_tensor_tensor(w12[:, :, 1], e2[:, :], 1.0 / Y_SCALE, w12[:, :, 0],
                                                        op0=ALU.mult, op1=ALU.mult), i, first)
                    link(nc.vector.tensor_scalar(w12[:, :, 0], w12[:, :, 0], 1.0 / Y_SCALE, None, ALU.mult), i, first)
                    for c in (0, 1):
                        for t in range(QT):
                            last = nc.vector.tensor_scalar(pick[:, c, t, :], iota[:, :], topf[:, t, c:c + 1], w12[:, t, c:c + 1],
                                                           ALU.is_equal, ALU.mult)
                    link(last, i, first)
                    link(nc.vector.tensor_tensor(pick[:, 0], pick[:, 0], pick[:, 1], ALU.add), i, first)
                elif kind == "norm_ctx":
                    k = misc_k((kind, l, n), first)
                    dve.wait_ge(misc_full.sem, misc_full.at(i, k))
                    src = ps_misc[:, 0:SEQ].rearrange("p (t c m) -> p t c m", t=QT, c=4)
                    link(nc.vector.reciprocal(rden[:, :, :], src[:, :, :, HEAD_DIM]), i, first)
                    dst = ctx_n[l][:, :, 4 * n * HEAD_DIM:4 * (n + 1) * HEAD_DIM].rearrange("p t (c d) -> p t c d", c=4)
                    nc.vector.tensor_tensor(dst, src[:, :, :, 0:HEAD_DIM],
                                            rden[:, :, :].unsqueeze(3).to_broadcast([128, QT, 4, HEAD_DIM]),
                                            ALU.mult).then_inc(misc_out.sem, 1)
                elif kind == "out":
                    k = misc_k((kind, l, n), first)
                    dve.wait_ge(misc_full.sem, misc_full.at(i, k))
                    src = ps_misc[:, 0:QT * HID].rearrange("p (t d) -> p t d", t=QT)
                    if l == 0:
                        dve.wait_ge(y_used.sem, y_used.at(i, MLPS))
                        nc.vector.tensor_tensor(x_mid[:, :, :], src, acc[:, :, :], ALU.add).then_inc(misc_out.sem, 1)
                    else:
                        dve.wait_ge(stored.sem, stored.at(i, 0))
                        nc.vector.tensor_tensor(y_out[:, :, :], src, res1[:, :, :], ALU.add).then_inc(misc_out.sem, 1)

            chain = sem("setup_chain")
            done = [0]

            def then(ins):
                done[0] += 1
                ins.then_inc(chain, 1)
                dve.wait_ge(chain, done[0])

            for s in (score_used[0], score_used[1], y_used, stored):
                dve.sem_inc(s.sem, 1)
            dve.sem_inc(a_done.sem, 2)
            for l in (0, 1):
                nc.vector.memset(V[l][:, :, :, :], 0.0)
            then(nc.vector.memset(x_mid[:, :, :], 0.0))
            for l in (0, 1):
                then(nc.vector.memset(V[l][:, :, :, HEAD_DIM:HEAD_DIM + 1], 1.0))
            dve.wait_ge(consts_in, CONSTS)
            then(nc.vector.tensor_scalar(slope32[:, :], slope32[:, :], SIGMA, None, ALU.mult))
            then(nc.vector.tensor_copy(slope_part[:, 0, :], slope32[:, :]))
            then(nc.vector.tensor_tensor(slope_rest[:, :], slope32[:, :], slope_part[:, 0, :], ALU.subtract))
            then(nc.vector.tensor_copy(slope_part[:, 1, :], slope_rest[:, :]))
            then(nc.vector.tensor_tensor(slope_part[:, 2, :], slope_rest[:, :], slope_part[:, 1, :], ALU.subtract))
            for r in range(3):
                last = nc.vector.tensor_copy(slope16[:, r, :].rearrange("p (h t) -> p h t", h=HEADS),
                                             slope_part[:, r, :].unsqueeze(2).to_broadcast([2, HEADS, SEQ]))
            last.then_inc(slopes_split, 1)
            for l in (0, 1):
                nc.vector.tensor_scalar(bcols[:, 2 * l:2 * l + 1], bcol[:, 2 * l:2 * l + 1], QK_SCALE / float(np.sqrt(HEAD_DIM)), None, ALU.mult)
                nc.vector.tensor_scalar(bcols[:, 2 * l + 1:2 * l + 2], bcol[:, 2 * l + 1:2 * l + 2], QK_SCALE, None, ALU.mult)
            then(nc.vector.tensor_tensor(brow[:, 3], brow[:, 3], brow[:, 5], ALU.add))
            then(nc.vector.tensor_scalar(brow[:, 4, 0, :], brow[:, 4, 0, :], 1.0 / 127.0, 1.0 / X_SCALE, ALU.mult, ALU.mult))
            then(nc.vector.tensor_tensor(cbs[:, :], cbs[:, :], brow[:, 4, 0, :], ALU.mult))
            nc.vector.memset(gap[:, :], 0.0).then_inc(weights_split, 1)
            for s in PREPARE[:-1]:
                stage(*s, 0, True)
            stage(*PREPARE[-1], 0, True)
            dve.wait_ge(weights_in, 32)
            for hi, lo, src in ((wgu[:, 0].rearrange("p m s f -> p (m s f)"), wgu[:, 1].rearrange("p m s f -> p (m s f)"), wgu32[:, :]),
                                (wd[:, 0].rearrange("p m f n -> p (m f n)"), wd[:, 1].rearrange("p m f n -> p (m f n)"), wd32[:, :])):
                then(nc.vector.tensor_scalar(hi, src, W_SCALE, None, ALU.mult))
                last = nc.vector.scalar_tensor_tensor(lo, src, W_SCALE, hi, op0=ALU.mult, op1=ALU.subtract)
            last.then_inc(weights_split, 1)
            assert marks[0] == DVE_LINKS_FIRST, marks
            marks[0] = 0
            with dve.Fori(0, TURNS) as i:
                for s in STAGES:
                    stage(*s, i, False)
            assert marks[0] == DVE_LINKS, marks

        @block.tensor
        def _(pe):
            def mlp_up(n, i):
                m, f = n // FT, n % FT
                rows = F_ROWS[f]
                pe.wait_ge(a_done.sem, a_done.at(i, n - 1))
                if n == 0:
                    pe.wait_ge(x_split.sem, x_split.at(i, 0))
                for side in (0, 1):
                    cols = slice(128 * f, 128 * f + rows)
                    for k, (w_half, x_half) in enumerate(((0, 0), (0, 1), (1, 0))):
                        last = nc.tensor.matmul(ps_gu[n % 2][:rows, side, :], wgu[:, w_half, m, side, cols], x16[:, x_half, :],
                                                start=(k == 0), stop=(k == 2))
                last.then_inc(gu_full.sem, 1)

            def mlp_down(n, i):
                m, f = n // FT, n % FT
                rows = F_ROWS[f]
                pe.wait_ge(lo_done.sem, lo_done.at(i, n + 1))
                if f == 0:
                    pe.wait_ge(y_used.sem, y_used.at(i, m))
                for t in range(QT):
                    for k, (a_half, w_half) in enumerate(((0, 0), (0, 1), (1, 0))):
                        last = nc.tensor.matmul(ps_y[:, 128 * t:128 * t + 128], a16[:rows, n % 4, a_half, 128 * t:128 * t + 128],
                                                wd[:rows, w_half, m, f, :], start=(f == 0 and t == 0 and k == 0),
                                                stop=(f == FT - 1 and k == 2), skip_group_check=True)
                if f == FT - 1:
                    last.then_inc(y_full.sem, 1)

            def scores(kind, l, n, i):
                k = score_at[(kind, l, n)]
                slot, place = (k - 1) % 2, (k - 1) // 2
                pe.wait_ge(score_used[slot].sem, score_used[slot].at(i, place))
                if n == 0 and kind == "max":
                    pe.wait_ge(qk_read[l].sem, qk_read[l].at(i, 96 * l))
                if n == 0 and kind == "exp":
                    pe.wait_ge(max_read[l].sem, max_read[l].at(i, 32))
                a, t = n // 2, n % 2
                at, whole, rows = (QS[l], KS[l], MAX_ROW) if kind == "max" else (KS[l], QS[l], MAX_ROW + 1)
                for g in (0, 1):
                    for j in (0, 1):
                        strip = slice(STRIP * j, STRIP * j + rows)
                        last = nc.tensor.matmul(ps_score[slot][:, j, g, :], at[strip, 2 * a + g, 128 * t:128 * t + 128],
                                                whole[strip, 2 * a + g, :], start=True, stop=True)
                last.then_inc(score_full.sem, 1)

            def stage(kind, l, n, i, first):
                if kind == "mlp":
                    if 0 <= n - 4 < UNITS:
                        mlp_down(n - 4, i)
                    if n < UNITS:
                        mlp_up(n, i)
                    return
                if kind in ("max", "exp"):
                    return scores(kind, l, n, i)
                if kind not in MISC:
                    return
                k = misc_k((kind, l, n), first)
                if not (first and k == 1 - P0):
                    pe.wait_ge(misc_out.sem, misc_out.at(i, k - 1))
                if kind == "xT":
                    pe.wait_ge(normed[l].sem, normed[l].at(i, 0 if first else 1))
                    for t in range(QT):
                        last = nc.tensor.transpose(ps_misc[:, 128 * t:128 * t + 128], xn[l][:, t, :], ident[:, :])
                elif kind == "qk":
                    pe.wait_ge(misc_out.sem, misc_out.at(i, misc_k(("xT", l, 0), first)))
                    for side in (0, 1):
                        last = nc.tensor.matmul(ps_misc[:, SEQ * side:SEQ * (side + 1)], wsq[:, 4 * l + side, :], xs[l][:, :],
                                                start=True, stop=True)
                elif kind == "v":
                    for t in range(QT):
                        last = nc.tensor.matmul(ps_misc[:, 128 * t:128 * t + 128], xs[l][:, 128 * t:128 * t + 128], wsq[:, 4 * l + 2, :],
                                                start=True, stop=True)
                elif kind == "router":
                    for t in range(QT):
                        last = nc.tensor.matmul(ps_misc[:, EXPERTS * t:EXPERTS * (t + 1)], xs[l][:, 128 * t:128 * t + 128], gates[:, :],
                                                start=True, stop=True)
                elif kind == "maxT":
                    for slot in (0, 1):
                        last_k = max(score_at[("max", l, m)] for m in range(8) if (score_at[("max", l, m)] - 1) % 2 == slot)
                        pe.wait_ge(score_used[slot].sem, score_used[slot].at(i, (last_k - 1) // 2 + 1))
                    for t in range(QT):
                        last = nc.tensor.transpose(ps_misc[0:HEADS, 128 * t:128 * t + 128], row_max[l][:, t, :], ident[:, :])
                elif kind == "pv":
                    for t in range(QT):
                        kk = score_at[("exp", l, 2 * n + t)]
                        pe.wait_ge(score_used[(kk - 1) % 2].sem, score_used[(kk - 1) % 2].at(i, (kk - 1) // 2 + 1))
                    buf = group_at[("exp", l, 2 * n)] % 2
                    for t in range(QT):
                        for c in range(4):
                            last = nc.tensor.matmul(ps_misc[32 * c:32 * c + 32, 0:SEQ], V[l][:, t, 4 * n + c, :],
                                                    prob[:, buf, t, c % 2, c // 2, :], start=(t == 0), stop=(t == QT - 1))
                elif kind == "norm_ctx":
                    pe.wait_ge(misc_out.sem, misc_out.at(i, misc_k(("pv", l, n), first)))
                    for t in range(QT):
                        last = nc.tensor.transpose(ps_misc[:, 128 * t:128 * t + 128], pv_sb[:, n % 2, 128 * t:128 * t + 128], ident[:, :])
                elif kind == "ctxT":
                    for t in range(QT):
                        last = nc.tensor.transpose(ps_misc[:, 128 * t:128 * t + 128], ctx_n[l][:, t, :], ident[:, :])
                elif kind == "out":
                    pe.wait_ge(misc_out.sem, misc_out.at(i, misc_k(("ctxT", l, 0), first)))
                    for t in range(QT):
                        dst = ps_misc[:, 128 * t:128 * t + 128]
                        last = nc.tensor.matmul(dst, ctx_t[l][:, 128 * t:128 * t + 128], wsq[:, 4 * l + 3, :], start=True, stop=(l == 0))
                        if l:
                            last = nc.tensor.matmul(dst, xs[1][:, 128 * t:128 * t + 128], cbs[:, :], start=False, stop=True)
                last.then_inc(misc_full.sem, 1)

            pe.wait_ge(consts_in, CONSTS)
            for s in PREPARE:
                stage(*s, 0, True)
            pe.wait_ge(weights_split, 2)
            pe.wait_ge(small_ready, 16 * 28)
            with pe.Fori(0, TURNS) as i:
                for s in STAGES:
                    stage(*s, i, False)


DVE_LINKS, DVE_LINKS_FIRST = 23, 12


def kernel(**inputs):
    import concourse.bacc as bacc
    from concourse.bass_utils import run_bass_kernel_spmd

    a = {k: np.asarray(v) for k, v in inputs.items()}
    c = np.ascontiguousarray

    def feat(w):
        return w

    x = a["L0_attn_x"].reshape(BATCHES, QT, 128, HID).transpose(0, 2, 1, 3)
    x = np.concatenate([x, np.zeros((TURNS + 1 - BATCHES,) + x.shape[1:], x.dtype)])
    w_gu = np.concatenate([a["L0_ffn_base_wgu"][None], a["L0_ffn_exp_wgu"]]).transpose(1, 0, 2).reshape(128, -1)
    w_d = np.concatenate([a["L0_ffn_base_wd"][None], a["L0_ffn_exp_wd"]])
    w_d = np.pad(w_d, ((0, 0), (0, FT * 128 - INTER), (0, 0))).reshape(MLPS, FT, 128, HID).transpose(2, 0, 1, 3).reshape(128, -1)
    w_sq = np.stack([a[f"L{l}_attn_W{n}"].T for l in (0, 1) for n in "qkvo"], 1)
    b_col = np.stack([a["L0_attn_bq"], a["L0_attn_bk"], a["L1_attn_bq"], a["L1_attn_bk"]], 1)
    rows = np.stack([a["L0_attn_bv"], a["L0_attn_bo"], a["L1_attn_bv"], a["L1_attn_bo"], a["L1_ffn_SCB"], a["L1_ffn_bias"]])
    b_row = np.broadcast_to(rows[None, :, None, :], (128, 6, QT, 128))
    slopes1 = -np.power(np.float32(2.0), np.linspace(-4.0, -0.3, HEADS, dtype=np.float32)).astype(np.float32)
    slopes = np.stack([a["L0_attn_slopes"], slopes1])
    pos = np.tile(np.arange(SEQ, dtype=np.float16), HEADS // 2)[None]
    arrays = {
        "x": c(x), "w_gu": c(w_gu), "w_down": c(w_d), "w_sq": c(w_sq), "cb": c(a["L1_ffn_CB"].T), "gate": c(a["L0_ffn_gate_w"]),
        "b_col": c(b_col), "b_row": c(b_row), "slopes": c(slopes), "pos": c(pos),
        "sigma_row": np.full_like(pos, SIGMA), "ident_in": np.eye(128, dtype=np.float32),
        "iota_in": c(np.broadcast_to(np.arange(EXPERTS, dtype=np.float32), (128, EXPERTS))),
    }
    nc = bacc.Bacc("TRN2", target_bir_lowering=False, num_devices=1)
    aps = [nc.dram_tensor(k, v.shape, mybir.dt.from_np(v.dtype), kind="ExternalInput").ap() for k, v in arrays.items()]
    out = nc.dram_tensor("out", (TURNS, 128, QT, HID), mybir.dt.float32, kind="ExternalOutput").ap()
    build(nc, *aps, out)
    r = run_bass_kernel_spmd(nc, [arrays], core_ids=[0])
    return r.results[0]["out"][1:].transpose(0, 2, 1, 3).reshape(BATCHES, SEQ, HID)
```

```python
import numpy as np
from contextlib import ExitStack

import concourse.bass as bass
from concourse import mybir

BATCHES, SEQ, HID = 32, 256, 128
HEADS = 16
HEAD_DIM = HID // HEADS
INTER = 352
EXPERTS = 8
MLPS = EXPERTS + 1
QT = SEQ // 128
FT = -(-INTER // 128)
F_ROWS = [min(128, INTER - 128 * f) for f in range(FT)]
UNITS = MLPS * FT
TURNS = BATCHES
EPS = 1e-5
DEPTH = 3

X_SCALE = 16.0
W_SCALE = 64.0
A_SCALE = 16.0
QK_SCALE = 32.0
SIGMA = QK_SCALE * QK_SCALE
GU_SCALE = X_SCALE * W_SCALE
Y_SCALE = A_SCALE * W_SCALE

STRIP = 64
PARTS = 8
MAX_ROW = PARTS * (HEAD_DIM - 1) + 3



HANDOVER = 15


def unit_of(w):
    u = (w - HANDOVER) % UNITS
    return u // FT, u % FT


ATTENTION = {
    0: ([("maxT", 0, 0)], [("pv", 1, 3), ("norm", 0, 0)]),
    1: ([("norm_ctx", 1, 3)], []),
    2: ([("max", 1, 0)], [("ctxT", 1, 0), ("xn", 0, 0), ("exp", 0, 0)]),
    3: ([("max", 1, 1)], [("out", 1, 0), ("exp", 0, 1)]),
    4: ([], [("pv", 0, 0), ("hold", 1, 0), ("xT", 0, 0)]),
    5: ([("max", 1, 2)], [("exp", 0, 2), ("norm_ctx", 0, 0)]),
    6: ([("max", 1, 3)], [("exp", 0, 3), ("qk", 0, 0)]),
    7: ([], [("pv", 0, 1), ("split_qk", 0, 0), ("v", 1, 0)]),
    8: ([("max", 1, 4)], [("exp", 0, 4), ("norm_ctx", 0, 1), ("strips", 0, 0)]),
    9: ([("max", 1, 5)], [("exp", 0, 5), ("router", 0, 0)]),
    10: ([], [("pv", 0, 2), ("e2", 0, 0), ("split_x", 0, 0)]),
    11: ([("max", 1, 6)], [("exp", 0, 6), ("norm_ctx", 0, 2), ("cw", 0, 0)]),
    12: ([("max", 1, 7)], [("exp", 0, 7)]),
    13: ([("maxT", 1, 0)], [("pv", 0, 3), ("strips2", 0, 0)]),
    14: ([("norm_ctx", 0, 3)], []),
    15: ([("max", 0, 0)], [("ctxT", 0, 0), ("exp", 1, 0)]),
    16: ([("max", 0, 1)], [("exp", 1, 1), ("v", 0, 0), ("keep_x", 0, 0)]),
    17: ([], [("pv", 1, 0)]),
    18: ([("max", 0, 2)], [("exp", 1, 2), ("norm_ctx", 1, 0)]),
    19: ([("max", 0, 3)], [("out", 0, 0), ("exp", 1, 3), ("start", 0, 0), ("load", 0, 0), ("norm", 1, 0)]),
    20: ([], [("pv", 1, 1), ("xn", 1, 0)]),
    21: ([("max", 0, 4)], [("exp", 1, 4), ("norm_ctx", 1, 1), ("xT", 1, 0)]),
    22: ([("max", 0, 5)], [("exp", 1, 5), ("qk", 1, 0)]),
    23: ([], [("pv", 1, 2), ("split_qk", 1, 0)]),
    24: ([("max", 0, 6)], [("exp", 1, 6), ("norm_ctx", 1, 2), ("strips", 1, 0)]),
    25: ([("max", 0, 7)], [("exp", 1, 7), ("dense", 1, 0)]),
    26: ([("strips2", 1, 0)], []),
}


def order_of_stages():
    s = []
    for w in range(UNITS):
        before = [(w - k) % UNITS for k in range(4)]
        one, two = ATTENTION[w]
        if unit_of(before[3])[1] == FT - 1:
            s.append(("y_read", 0, before[3]))
        up, gate = ("up", 0, w), ("gate_u", 0, before[1])
        s += [up, gate] if w else [gate, up]
        s += [("tanh", 0, w)] + one + [("gate_g", 0, w), ("high", 0, before[1]), ("low", 0, before[1])]
        s += two[:1] + [("down", 0, before[2])] + two[1:]
    return s


STAGES = order_of_stages()
PIPE = ("up", "high", "tanh", "gate_g", "gate_u", "low", "down", "y_read")


def ahead_of_turns():
    keep, window = [], 0
    for s in STAGES:
        kind, l, n = s
        if kind in ("up",):
            window = n
        if kind in PIPE:
            u = (n - HANDOVER) % UNITS
            if n >= HANDOVER and window >= HANDOVER:
                keep.append(s)
        elif kind == "max" and l == 0:
            keep.append(s)
        elif l == 0 and kind in ("norm", "xn", "xT", "qk", "split_qk", "router", "e2", "cw", "strips", "strips2", "v", "start", "load", "split_x", "keep_x"):
            keep.append(s)
    return keep


TAIL = [("pv", 1, 3), ("norm_ctx", 1, 3), ("ctxT", 1, 0), ("out", 1, 0)]
FIRST = ahead_of_turns()
LAST = [s for s in STAGES if s[1] == 1 and s[0] in ("max", "exp", "pv", "norm_ctx", "ctxT", "out", "hold", "v", "maxT")]
END = TAIL
PROGRAMS = {"first": FIRST, "turn": STAGES, "last": LAST, "end": END}
MISC = ("xT", "qk", "v", "router", "maxT", "pv", "norm_ctx", "ctxT", "out", "dense")
RANK = {name: {s: n for n, s in enumerate(p)} for name, p in PROGRAMS.items()}
LINKS = {"norm": 2, "router": 3, "cw": 5, "norm_ctx": 1, "split_x": 1}


class Signal:

    def __init__(self, sem, signals):
        self.sem, self.signals = sem, signals
        self.done, total = {}, {}
        for name, program in PROGRAMS.items():
            count, self.done[name] = 0, {}
            for s in program:
                count += signals(s)
                self.done[name][s] = count
            total[name] = count
        self.per = total["turn"]
        self.prime = self.per - total["first"]
        after_loop = self.per * (TURNS + 1)
        self.base = {"first": self.prime, "last": after_loop, "end": after_loop + total["last"]}
        self.total = after_loop + total["last"] + total["end"]

    def before(self, turn, here):
        return self.at(turn, here, here, self.signals(here))

    def at(self, turn, here, stage, short=0):
        name = turn if isinstance(turn, str) else "turn"
        rank = RANK[name]
        this = stage in rank and rank[stage] <= rank[here]
        if isinstance(turn, str):
            return self.base[name] + (self.done[name][stage] - short if this else 0)
        return (turn + (1 if this else 0)) * self.per + (self.done[name][stage] - short)


def of(*kinds, layer=None, number=1):
    return lambda s: number if s[0] in kinds and layer in (None, s[1]) else 0


def build(nc, x, w_gu, w_down, w_sq, cb, gate, b_col, b_row, slopes, parts, k_rows, ident_in, iota_in, out):
    f32, f16, u32 = mybir.dt.float32, mybir.dt.float16, mybir.dt.uint32
    ALU, ACT, AX = mybir.AluOpType, mybir.ActivationFunctionType, mybir.AxisListType
    with ExitStack() as ctx:
        def sb(name, shape, dt=f32):
            return ctx.enter_context(nc.sbuf_tensor(name, shape, dt))

        def sem(name):
            return ctx.enter_context(nc.semaphore(name))

        wgu32 = sb("wgu32", [128, MLPS * 2 * INTER])
        wd32 = sb("wd32", [128, MLPS * FT * 128])
        wgu = sb("wgu", [128, 2, MLPS, 2, INTER], f16)
        wd = sb("wd", [128, 2, MLPS, FT, 128], f16)
        wsq = sb("wsq", [128, 8, 128])
        cbs = sb("cbs", [128, 128])
        gates = sb("gates", [128, EXPERTS])
        bcol = sb("bcol", [128, 6])
        bcols = sb("bcols", [128, 4])
        brow = sb("brow", [128, 4, QT, 128])
        bv_cols = sb("bv_cols", [128, 2, 128])
        ident = sb("ident", [128, 128])
        iota = sb("iota", [128, EXPERTS])
        slope32, slope_rest = sb("slope32", [128, 2, HEADS // 2]), sb("slope_rest", [128, 2, HEADS // 2])
        slope_part, slope_row = sb("slope_part", [128, 3, 2, HEADS // 2], f16), sb("slope_row", [128, 2, HEADS // 2])
        part_mask = sb("part_mask", [128, 3])
        x_in = sb("x_in", [128, QT, HID])
        acc = sb("acc", [128, QT, HID])
        x_mid = sb("x_mid", [128, QT, HID])
        res1 = sb("res1", [128, QT, HID])
        res_hold = sb("res_hold", [128, QT, HID])
        y_out = sb("y_out", [128, QT, HID])
        x16 = [sb("x16_late", [128, 2, SEQ], f16), sb("x16_early", [128, 2, SEQ], f16)]
        both = lambda name, shape, dt=f32: [sb(f"{name}{l}", shape, dt) for l in (0, 1)]
        stats, mv, rstd = both("stats", [128, QT, 6]), both("mv", [128, QT, 2]), both("rstd", [128, QT])
        var = both("var", [128, QT])
        minus_half = sb("minus_half", [128, QT])
        xn, xs = both("xn", [128, QT, HID]), both("xs", [128, SEQ])
        qk32, qk16 = both("qk32", [128, 2, SEQ]), both("qk16", [128, 2, 2, SEQ], f16)
        strips1, strips2 = both("strips1_", [128, 2, HEADS // 2, SEQ], f16), both("strips2_", [128, 2, HEADS // 2, SEQ], f16)
        V = both("V", [128, QT, HEADS, 32])
        row_max, max_t = both("row_max", [128, QT, HEADS]), both("max_t", [HEADS, SEQ], f16)
        ctx_n, ctx_t = both("ctx_n", [128, QT, HID]), both("ctx_t", [128, SEQ])
        prob = sb("prob", [128, 2, QT, 2, 2, SEQ])
        pv_sb = sb("pv_sb", [128, 2, SEQ])
        rden = sb("rden", [128, QT, 4])
        tanh_sb, gated = sb("tanh_sb", [128, FT, SEQ]), sb("gated", [128, FT, SEQ])
        a32 = sb("a32", [128, DEPTH, SEQ])
        a16 = sb("a16", [128, DEPTH, 2, SEQ], f16)
        y_sb = sb("y_sb", [128, QT, HID])
        logit = sb("logit", [128, QT, EXPERTS])
        top = sb("top", [128, QT, 8])
        topi = sb("topi", [128, QT, 8], u32)
        topf = sb("topf", [128, QT, 2])
        gap, e2, den = sb("gap", [128, QT]), sb("e2", [128, QT]), sb("den", [128, QT])
        w12 = sb("w12", [128, QT, 2])
        pick = sb("pick", [128, 2, QT, EXPERTS])
        cw = sb("cw", [128, QT, EXPERTS])

        ps_max = ctx.enter_context(nc.psum_tensor("ps_max", [128, 2, 2, SEQ], f32))
        ps_exp = ctx.enter_context(nc.psum_tensor("ps_exp", [128, 2, 2, SEQ], f32))
        ps_gu = [ctx.enter_context(nc.psum_tensor(f"ps_gu{n}", [128, 2, SEQ], f32)) for n in (0, 1)]
        ps_y = ctx.enter_context(nc.psum_tensor("ps_y", [128, 512], f32))
        ps_misc = ctx.enter_context(nc.psum_tensor("ps_misc", [128, 512], f32))

        scratch = [nc.dram_tensor(f"scratch{l}", [2, 2, 128, SEQ], f16, kind="Internal").ap() for l in (0, 1)]

        consts_in, weights_in, x_first = sem("consts_in"), sem("weights_in"), sem("x_first")
        cleared, rows_in = sem("cleared"), sem("rows_in")
        bv_spread, bv_out, biases_ready, weights_split = sem("bv_spread"), sem("bv_out"), sem("biases_ready"), sem("weights_split")

        by_stage = []

        def signal(name, *kinds, layer=None, number=1):
            by_stage.append(Signal(sem(name), of(*kinds, layer=layer, number=number)))
            return by_stage[-1]

        misc_full = signal("misc_full", *MISC)
        misc_out = signal("misc_out", *MISC)
        max_full = signal("max_full", "max")
        max_used = signal("max_used", "max")
        exp_full = signal("exp_full", "exp")
        exp_used = signal("exp_used", "exp")
        gu_full = signal("gu_full", "up")
        tanh_done = signal("tanh_done", "tanh")
        gated_done = signal("gated_done", "gate_g")
        a_done = signal("a_done", "gate_u")
        hi_done = signal("hi_done", "high")
        lo_done = signal("lo_done", "low")
        y_full = Signal(sem("y_full"), lambda s: int(s[0] == "down" and unit_of(s[2])[1] == FT - 1))
        by_stage.append(y_full)
        y_read = signal("y_read", "y_read")
        y_added = signal("y_added", "y_read")
        acc_set = signal("acc_set", "start")
        cw_set = signal("cw_set", "start")
        x_loaded = signal("x_loaded", "load", number=16)
        var_done = signal("var_done", "norm")
        rstd_done = signal("rstd_done", "norm")
        res_set = signal("res_set", "norm", layer=1)
        held = signal("held", "hold")
        normed = signal("normed", "xn")
        x_split = signal("x_split", "split_x")
        x_kept = signal("x_kept", "keep_x")
        qk_high = signal("qk_high", "split_qk")
        qk_low = signal("qk_low", "split_qk")
        qk_written = signal("qk_written", "split_qk", number=16)
        qk_read = [signal(f"qk_read{l}", "strips", layer=l, number=96) for l in (0, 1)]
        copied = [signal(f"copied{l}", "strips2", layer=l, number=16) for l in (0, 1)]
        max_read = [signal(f"max_read{l}", "maxT", layer=l, number=32) for l in (0, 1)]
        gap_ready = signal("gap_ready", "router")
        e2_ready = signal("e2_ready", "e2")
        stored = signal("stored", "out", layer=1, number=16)
        dve_link = Signal(sem("dve_link"), lambda s: LINKS.get(s[0], 0))
        by_stage.append(dve_link)
        CONSTS = 16 * 9

        def run(engine, stage):
            for s in FIRST:
                stage(*s, "first")
            for g in by_stage:
                engine.wait_ge(g.sem, g.per)
            with engine.Fori(0, TURNS) as i:
                for s in STAGES:
                    stage(*s, i)
            for g in by_stage:
                engine.wait_ge(g.sem, g.base["last"])
            for s in LAST:
                stage(*s, "last")
            for g in by_stage:
                engine.wait_ge(g.sem, g.base["end"])
            for s in END:
                stage(*s, "end")

        block = ctx.enter_context(nc.Block())

        @block.sync
        def _(sp):
            for g in by_stage:
                if g.prime:
                    sp.sem_inc(g.sem, g.prime)
            for dst, src in ((wsq[:, :, :], w_sq), (gates[:, :], gate), (bcol[:, :], b_col), (ident[:, :], ident_in),
                             (iota[:, :], iota_in), (brow[:, :, :, :], b_row), (cbs[:, :], cb), (slope32[:, :, :], slopes),
                             (part_mask[:, :], parts)):
                sp.dma_start(dst, src).then_inc(consts_in, 16)
            sp.dma_start(x_in[:, :, :], x[0]).then_inc(x_first, 16)
            sp.dma_start(wgu32[:, :], w_gu).then_inc(weights_in, 16)
            sp.dma_start(wd32[:, :], w_down).then_inc(weights_in, 16)
            for l in (0, 1):
                for strips in (strips1[l], strips2[l]):
                    sp.dma_start(strips[:, 1, :, :], k_rows).then_inc(rows_in, 16)

            def number(value):
                return value if isinstance(value, int) else sp.to_reg(value)

            def wait_first(signal, turn, here, stage):
                value = signal.at(turn, here, stage)
                if not isinstance(value, int):
                    value = sp.to_reg(value)
                    sp.wait_ge(cleared, 1)
                sp.wait_ge(signal.sem, value)

            def stage(kind, l, n, turn):
                here = (kind, l, n)
                if kind == "load":
                    wait_first(acc_set, turn, here, ("start", 0, 0))
                    batch = 1 if isinstance(turn, str) else turn + 2
                    sp.dma_start(x_in[:, :, :], x[batch]).then_inc(x_loaded.sem, 16)
                elif kind == "split_qk":
                    sp.wait_ge(qk_low.sem, qk_low.at(turn, here, here))
                    sp.dma_start(scratch[l].rearrange("a s p t -> p a s t"), qk16[l][:, :, :, :]).then_inc(qk_written.sem, 16)
                elif kind == "strips":
                    through = number(max_full.at(turn, here, ("max", l, 7)))
                    written, kept = number(qk_written.at(turn, here, ("split_qk", l, 0))), number(copied[l].at(turn, here, ("strips2", l, 0)))
                    sp.wait_ge(max_full.sem, through)
                    sp.wait_ge(copied[l].sem, kept)
                    sp.wait_ge(qk_written.sem, written)
                    for side, halves in ((0, (0, 0, 1)), (1, (0, 1, 0))):
                        for r, half in enumerate(halves):
                            sp.dma_start(strips1[l][r:128:PARTS, side, :, :],
                                         scratch[l][half, side].rearrange("(g p) t -> p g t", p=16)).then_inc(qk_read[l].sem, 16)
                elif kind == "strips2":
                    through, there = number(exp_full.at(turn, here, ("exp", l, 7))), number(qk_read[l].at(turn, here, ("strips", l, 0)))
                    sp.wait_ge(exp_full.sem, through)
                    sp.wait_ge(qk_read[l].sem, there)
                    sp.dma_start(strips2[l][:, :, :, :], strips1[l][:, :, :, :]).then_inc(copied[l].sem, 16)
                elif kind == "maxT":
                    there, copy = number(misc_out.at(turn, here, here)), number(copied[l].at(turn, here, ("strips2", l, 0)))
                    sp.wait_ge(misc_out.sem, there)
                    sp.wait_ge(copied[l].sem, copy)
                    for j in (0, 1):
                        row = STRIP * j + MAX_ROW
                        sp.dma_start(strips2[l][row:row + 1, 0, :, :], max_t[l][j:HEADS:2, :]).then_inc(max_read[l].sem, 16)
                elif kind == "out" and l == 1:
                    wait_first(misc_out, turn, here, here)
                    batch = {"last": TURNS, "end": TURNS + 1}[turn] if isinstance(turn, str) else turn
                    sp.dma_start(out[batch], y_out[:, :, :]).then_inc(stored.sem, 16)

            run(sp, stage)
            sp.wait_ge(stored.sem, stored.total)
            sp.wait_ge(qk_written.sem, qk_written.total)

        @block.gpsimd
        def _(pool):
            nc.gpsimd.memset(minus_half[:, :], -0.5).then_inc(cleared, 1)
            pool.wait_ge(cleared, 1)
            pool.wait_ge(biases_ready, 1)
            pool.wait_ge(x_first, 16)

            def stage(kind, l, n, turn):
                here = (kind, l, n)
                if kind == "low":
                    rows, b = F_ROWS[unit_of(n)[1]], n % DEPTH
                    pool.wait_ge(hi_done.sem, hi_done.at(turn, here, ("high", 0, n)))
                    nc.gpsimd.tensor_tensor(a16[:rows, b, 1, :], a32[:rows, b, :], a16[:rows, b, 0, :],
                                            ALU.subtract).then_inc(lo_done.sem, 1)
                elif kind == "norm":
                    pool.wait_ge(var_done.sem, var_done.at(turn, here, here))
                    nc.gpsimd.tensor_tensor(rstd[l][:, :], var[l][:, :], minus_half[:, :], ALU.pow).then_inc(rstd_done.sem, 1)
                    if l:
                        pool.wait_ge(held.sem, held.at(turn, here, ("hold", 1, 0)))
                        nc.gpsimd.tensor_tensor(res1[:, :, :], x_mid[:, :, :], brow[:, 1], ALU.add).then_inc(res_set.sem, 1)
                elif kind == "split_qk":
                    pool.wait_ge(qk_high.sem, qk_high.at(turn, here, here))
                    nc.gpsimd.tensor_tensor(qk16[l][:, 1], qk32[l][:, :, :], qk16[l][:, 0], ALU.subtract).then_inc(qk_low.sem, 1)
                elif kind == "start":
                    pool.wait_ge(misc_out.sem, misc_out.at(turn, here, ("out", 0, 0)))
                    if not isinstance(turn, str):
                        pool.wait_ge(x_loaded.sem, x_loaded.at(turn, here, ("load", 0, 0)))
                    nc.gpsimd.tensor_tensor(acc[:, :, :], x_in[:, :, :], brow[:, 0], ALU.add).then_inc(acc_set.sem, 1)
                elif kind == "y_read":
                    pool.wait_ge(y_read.sem, y_read.at(turn, here, here))
                    pool.wait_ge(acc_set.sem, acc_set.at(turn, here, ("start", 0, 0)))
                    pool.wait_ge(y_added.sem, y_added.before(turn, here))
                    nc.gpsimd.tensor_tensor(acc[:, :, :], acc[:, :, :], y_sb[:, :, :], ALU.add).then_inc(y_added.sem, 1)

            run(pool, stage)

        @block.scalar
        def _(act):
            act.wait_ge(biases_ready, 1)

            def stage(kind, l, n, turn):
                here = (kind, l, n)
                if kind == "high":
                    rows, b = F_ROWS[unit_of(n)[1]], n % DEPTH
                    act.wait_ge(a_done.sem, a_done.at(turn, here, ("gate_u", 0, n)))
                    nc.scalar.activation(a16[:rows, b, 0, :], a32[:rows, b, :], ACT.Copy).then_inc(hi_done.sem, 1)
                elif kind == "tanh":
                    rows = F_ROWS[unit_of(n)[1]]
                    act.wait_ge(gu_full.sem, gu_full.at(turn, here, ("up", 0, n)))
                    nc.scalar.activation(tanh_sb[:rows, n % FT, :], ps_gu[n % 2][:rows, 0, :], ACT.Tanh,
                                         scale=0.5 / GU_SCALE).then_inc(tanh_done.sem, 1)
                elif kind == "y_read":
                    m = unit_of(n)[0]
                    act.wait_ge(y_full.sem, y_full.at(turn, here, ("down", 0, n)))
                    act.wait_ge(y_added.sem, y_added.before(turn, here))
                    if m:
                        act.wait_ge(cw_set.sem, cw_set.at(turn, here, ("start", 0, 0)))
                    for t in range(QT):
                        by = cw[:, t, m - 1:m] if m else 1.0 / Y_SCALE
                        last = nc.scalar.activation(y_sb[:, t, :], ps_y[:, 128 * t:128 * t + 128], ACT.Copy, scale=by)
                    last.then_inc(y_read.sem, 1)
                elif kind == "exp":
                    act.wait_ge(exp_full.sem, exp_full.at(turn, here, here))
                    nc.scalar.activation(prob[:, n // 2 % 2, n % 2], ps_exp[:, :, :, :], ACT.Exp,
                                         scale=1.0 / SIGMA).then_inc(exp_used.sem, 1)
                elif kind in ("xT", "qk", "v", "maxT", "pv", "ctxT"):
                    act.wait_ge(misc_full.sem, misc_full.at(turn, here, here))
                    if kind == "xT":
                        last = nc.scalar.activation(xs[l][:, :], ps_misc[:, 0:SEQ], ACT.Copy, scale=X_SCALE)
                    elif kind == "qk":
                        nc.scalar.activation(qk32[l][:, 0, :], ps_misc[:, 0:SEQ], ACT.Identity, bias=bcols[:, 2 * l:2 * l + 1],
                                             scale=QK_SCALE / X_SCALE / float(np.sqrt(HEAD_DIM)))
                        last = nc.scalar.activation(qk32[l][:, 1, :], ps_misc[:, SEQ:2 * SEQ], ACT.Identity,
                                                    bias=bcols[:, 2 * l + 1:2 * l + 2], scale=QK_SCALE / X_SCALE)
                    elif kind == "v":
                        last = nc.scalar.activation(V[l][:, :, :, 0:HEAD_DIM],
                                                    ps_misc[:, 0:QT * HID].rearrange("p (t h d) -> p t h d", t=QT, d=HEAD_DIM),
                                                    ACT.Copy, scale=1.0 / X_SCALE)
                    elif kind == "maxT":
                        last = nc.scalar.activation(max_t[l][:, :], ps_misc[0:HEADS, 0:SEQ], ACT.Copy, scale=-1.0 / SIGMA)
                    elif kind == "pv":
                        last = nc.scalar.activation(pv_sb[:, n % 2, :], ps_misc[:, 0:SEQ], ACT.Copy)
                    else:
                        last = nc.scalar.activation(ctx_t[l][:, :], ps_misc[:, 0:SEQ], ACT.Copy)
                    last.then_inc(misc_out.sem, 1)
                elif kind == "e2":
                    act.wait_ge(gap_ready.sem, gap_ready.at(turn, here, ("router", 0, 0)))
                    nc.scalar.activation(e2[:, :], gap[:, :], ACT.Exp).then_inc(e2_ready.sem, 1)

            run(act, stage)

        @block.vector
        def _(dve):
            def number(value):
                return value if isinstance(value, int) else dve.to_reg(value)

            def stage(kind, l, n, turn):
                here = (kind, l, n)
                own = [dve_link.signals(here)]

                def link(ins, plain=False):
                    own[0] -= 1
                    ins.then_inc(dve_link.sem, 1)
                    value = number(dve_link.at(turn, here, here, own[0]))
                    if plain:
                        dve.wait_ge(consts_in, CONSTS)
                    dve.wait_ge(dve_link.sem, value)

                if kind == "start":
                    dve.wait_ge(y_read.sem, y_read.at(turn, here, ("y_read", 0, HANDOVER - 1)))
                    nc.vector.tensor_copy(cw[:, :, :], pick[:, 0]).then_inc(cw_set.sem, 1)
                elif kind == "norm":
                    src = x_mid if l else x_in
                    if l:
                        dve.wait_ge(misc_out.sem, misc_out.at(turn, here, ("out", 0, 0)))
                    elif isinstance(turn, str):
                        dve.wait_ge(x_first, 16)
                    else:
                        dve.wait_ge(x_loaded.sem, x_loaded.at(turn, here, ("load", 0, 0)))
                    for t in range(QT):
                        last = nc.vector.bn_stats(stats[l][:, t, :], src[:, t, :])
                    link(last, plain=True)
                    for t in range(QT):
                        last = nc.vector.bn_aggr(mv[l][:, t, :], stats[l][:, t, :])
                    link(last)
                    nc.vector.tensor_scalar(var[l][:, :], mv[l][:, :, 1], EPS, None, ALU.add).then_inc(var_done.sem, 1)
                elif kind == "xn":
                    src = x_mid if l else x_in
                    dve.wait_ge(rstd_done.sem, rstd_done.at(turn, here, ("norm", l, 0)))
                    for t in range(QT):
                        last = nc.vector.tensor_scalar(xn[l][:, t, :], src[:, t, :], mv[l][:, t, 0:1], rstd[l][:, t:t + 1],
                                                       ALU.subtract, ALU.mult)
                    last.then_inc(normed.sem, 1)
                elif kind == "max":
                    dve.wait_ge(max_full.sem, max_full.at(turn, here, here))
                    a, t = n // 2, n % 2
                    dst = row_max[l][:, t, 4 * a:4 * a + 4].rearrange("p (g j) -> p j g", j=2)
                    nc.vector.tensor_reduce(dst, ps_max[:, :, :, :], axis=AX.X, op=ALU.max).then_inc(max_used.sem, 1)
                elif kind == "gate_g":
                    rows = F_ROWS[unit_of(n)[1]]
                    dve.wait_ge(tanh_done.sem, tanh_done.at(turn, here, ("tanh", 0, n)))
                    nc.vector.scalar_tensor_tensor(gated[:rows, n % FT, :], tanh_sb[:rows, n % FT, :], 1.0,
                                                   ps_gu[n % 2][:rows, 0, :], op0=ALU.add, op1=ALU.mult).then_inc(gated_done.sem, 1)
                elif kind == "gate_u":
                    rows = F_ROWS[unit_of(n)[1]]
                    dve.wait_ge(gated_done.sem, gated_done.at(turn, here, ("gate_g", 0, n)))
                    nc.vector.scalar_tensor_tensor(a32[:rows, n % DEPTH, :], gated[:rows, n % FT, :], 0.5 * A_SCALE / GU_SCALE ** 2,
                                                   ps_gu[n % 2][:rows, 1, :], op0=ALU.mult, op1=ALU.mult).then_inc(a_done.sem, 1)
                elif kind == "split_qk":
                    dve.wait_ge(misc_out.sem, misc_out.at(turn, here, ("qk", l, 0)))
                    nc.vector.tensor_copy(qk16[l][:, 0], qk32[l][:, :, :]).then_inc(qk_high.sem, 1)
                elif kind == "split_x":
                    dve.wait_ge(x_kept.sem, x_kept.at(turn, here, ("keep_x", 0, 0)))
                    dve.wait_ge(gu_full.sem, gu_full.at(turn, here, ("up", 0, UNITS - 1)))
                    dve.wait_ge(misc_out.sem, misc_out.at(turn, here, ("xT", 0, 0)))
                    link(nc.vector.tensor_copy(x16[0][:, 0, :], xs[0][:, :]))
                    nc.vector.tensor_tensor(x16[0][:, 1, :], xs[0][:, :], x16[0][:, 0, :], ALU.subtract).then_inc(x_split.sem, 1)
                elif kind == "keep_x":
                    dve.wait_ge(gu_full.sem, gu_full.at(turn, here, ("up", 0, HANDOVER - 1)))
                    dve.wait_ge(x_split.sem, x_split.at(turn, here, ("split_x", 0, 0)))
                    nc.vector.tensor_copy(x16[1][:, :, :], x16[0][:, :, :]).then_inc(x_kept.sem, 1)
                elif kind == "router":
                    dve.wait_ge(misc_full.sem, misc_full.at(turn, here, here))
                    nc.vector.tensor_scalar(logit[:, :, :], ps_misc[:, 0:QT * EXPERTS].rearrange("p (t e) -> p t e", t=QT),
                                            1.0 / X_SCALE, None, ALU.mult).then_inc(misc_out.sem, 1)
                    value = number(misc_out.at(turn, here, here))
                    dve.wait_ge(consts_in, CONSTS)
                    dve.wait_ge(misc_out.sem, value)
                    for t in range(QT):
                        last = nc.vector.max(top[:, t, :], logit[:, t, :])
                    link(last)
                    nc.vector.tensor_tensor(gap[:, :], top[:, :, 1], top[:, :, 0], ALU.subtract).then_inc(gap_ready.sem, 1)
                    for t in range(QT):
                        last = nc.vector.max_index(topi[:, t, :], top[:, t, :], logit[:, t, :])
                    link(last)
                    link(nc.vector.tensor_copy(topf[:, :, :], topi[:, :, 0:2]))
                elif kind == "cw":
                    dve.wait_ge(e2_ready.sem, e2_ready.at(turn, here, ("e2", 0, 0)))
                    link(nc.vector.tensor_scalar(den[:, :], e2[:, :], 1.0, Y_SCALE, ALU.add, ALU.mult))
                    link(nc.vector.reciprocal(w12[:, :, 0], den[:, :]))
                    link(nc.vector.tensor_tensor(w12[:, :, 1], e2[:, :], w12[:, :, 0], ALU.mult))
                    for c in (0, 1):
                        for t in range(QT):
                            last = nc.vector.tensor_scalar(pick[:, c, t, :], iota[:, :], topf[:, t, c:c + 1], w12[:, t, c:c + 1],
                                                           ALU.is_equal, ALU.mult)
                    link(last)
                    link(nc.vector.tensor_tensor(pick[:, 0], pick[:, 0], pick[:, 1], ALU.add))
                elif kind == "norm_ctx":
                    dve.wait_ge(misc_full.sem, misc_full.at(turn, here, here))
                    src = ps_misc[:, 0:SEQ].rearrange("p (t c m) -> p t c m", t=QT, c=4)
                    link(nc.vector.reciprocal(rden[:, :, :], src[:, :, :, HEAD_DIM]))
                    dst = ctx_n[l][:, :, 4 * n * HEAD_DIM:4 * (n + 1) * HEAD_DIM].rearrange("p t (c d) -> p t c d", c=4)
                    nc.vector.tensor_tensor(dst, src[:, :, :, 0:HEAD_DIM],
                                            rden[:, :, :].unsqueeze(3).to_broadcast([128, QT, 4, HEAD_DIM]),
                                            ALU.mult).then_inc(misc_out.sem, 1)
                elif kind == "hold":
                    dve.wait_ge(misc_out.sem, misc_out.at(turn, here, ("out", 1, 0)))
                    nc.vector.tensor_copy(res_hold[:, :, :], res1[:, :, :]).then_inc(held.sem, 1)
                elif kind in ("out", "dense"):
                    dve.wait_ge(misc_full.sem, misc_full.at(turn, here, here))
                    src = ps_misc[:, 0:QT * HID].rearrange("p (t d) -> p t d", t=QT)
                    if kind == "dense":
                        dve.wait_ge(res_set.sem, res_set.at(turn, here, ("norm", 1, 0)))
                        last = nc.vector.tensor_tensor(res1[:, :, :], src, res1[:, :, :], ALU.add)
                    elif l == 0:
                        dve.wait_ge(y_added.sem, y_added.at(turn, here, ("y_read", 0, HANDOVER - 1)))
                        last = nc.vector.tensor_tensor(x_mid[:, :, :], src, acc[:, :, :], ALU.add)
                    else:
                        dve.wait_ge(held.sem, held.at(turn, here, ("hold", 1, 0)))
                        dve.wait_ge(stored.sem, stored.before(turn, here))
                        last = nc.vector.tensor_tensor(y_out[:, :, :], src, res_hold[:, :, :], ALU.add)
                    last.then_inc(misc_out.sem, 1)

            chain = sem("setup_chain")
            done = [0]

            def then(ins):
                done[0] += 1
                ins.then_inc(chain, 1)
                dve.wait_ge(chain, done[0])

            dve.wait_ge(consts_in, CONSTS)
            then(nc.vector.tensor_scalar(slope32[:, :, :], slope32[:, :, :], SIGMA, None, ALU.mult))
            then(nc.vector.tensor_copy(slope_part[:, 0], slope32[:, :, :]))
            then(nc.vector.tensor_tensor(slope_rest[:, :, :], slope32[:, :, :], slope_part[:, 0], ALU.subtract))
            then(nc.vector.tensor_copy(slope_part[:, 1], slope_rest[:, :, :]))
            then(nc.vector.tensor_tensor(slope_part[:, 2], slope_rest[:, :, :], slope_part[:, 1], ALU.subtract))
            then(nc.vector.tensor_scalar(slope_row[:, :, :], slope_part[:, 0], part_mask[:, 0:1], None, ALU.mult))
            for r in (1, 2):
                then(nc.vector.scalar_tensor_tensor(slope_row[:, :, :], slope_part[:, r], part_mask[:, r:r + 1], slope_row[:, :, :],
                                                    op0=ALU.mult, op1=ALU.add))
            for l in (0, 1):
                for strips in (strips1[l], strips2[l]):
                    nc.vector.tensor_copy(strips[:, 0, :, :], slope_row[:, l, :].unsqueeze(2).to_broadcast([128, HEADS // 2, SEQ]))
            for l in (0, 1):
                last = nc.vector.tensor_copy(bv_cols[:, l, :], bcol[:, 4 + l:5 + l].to_broadcast([128, 128]))
            last.then_inc(bv_spread, 1)
            for l in (0, 1):
                nc.vector.tensor_scalar(bcols[:, 2 * l:2 * l + 1], bcol[:, 2 * l:2 * l + 1], QK_SCALE / float(np.sqrt(HEAD_DIM)), None, ALU.mult)
                nc.vector.tensor_scalar(bcols[:, 2 * l + 1:2 * l + 2], bcol[:, 2 * l + 1:2 * l + 2], QK_SCALE, None, ALU.mult)
            then(nc.vector.tensor_tensor(brow[:, 1], brow[:, 1], brow[:, 3], ALU.add))
            then(nc.vector.tensor_scalar(brow[:, 2, 0, :], brow[:, 2, 0, :], 1.0 / 127.0, 1.0 / X_SCALE, ALU.mult, ALU.mult))
            nc.vector.tensor_tensor(cbs[:, :], cbs[:, :], brow[:, 2, 0, :], ALU.mult)
            dve.wait_ge(bv_out, 1)
            for l in (0, 1):
                for t in range(QT):
                    last = nc.vector.tensor_tensor(brow[:, l, t, :], ps_misc[:, 128 * l:128 * l + 128], brow[:, l, t, :], ALU.add)
            last.then_inc(biases_ready, 1)
            for tile in (res1[:, :, :], res_hold[:, :, :], ctx_n[1][:, :, :], xs[1][:, :]):
                nc.vector.memset(tile, 0.0)
            nc.vector.memset(prob[:, :, :, :, :, :], 1.0)
            for l in (0, 1):
                last = nc.vector.memset(V[l][:, :, :, :], 0.0)
            then(last)
            for l in (0, 1):
                last = nc.vector.memset(V[l][:, :, :, HEAD_DIM:HEAD_DIM + 1], 1.0)
            dve.wait_ge(weights_in, 32)
            for hi, lo, src in ((wgu[:, 0].rearrange("p m s f -> p (m s f)"), wgu[:, 1].rearrange("p m s f -> p (m s f)"), wgu32[:, :]),
                                (wd[:, 0].rearrange("p m f n -> p (m f n)"), wd[:, 1].rearrange("p m f n -> p (m f n)"), wd32[:, :])):
                then(nc.vector.tensor_scalar(hi, src, W_SCALE, None, ALU.mult))
                last = nc.vector.scalar_tensor_tensor(lo, src, W_SCALE, hi, op0=ALU.mult, op1=ALU.subtract)
            last.then_inc(weights_split, 1)
            run(dve, stage)

        @block.tensor
        def _(pe):
            def stage(kind, l, n, turn):
                here = (kind, l, n)
                if kind == "up":
                    m, f = unit_of(n)
                    rows = F_ROWS[f]
                    before = n - 2 if n >= 2 else UNITS - 1 - n
                    pe.wait_ge(a_done.sem, a_done.at(turn, here, ("gate_u", 0, before)))
                    if n == HANDOVER:
                        pe.wait_ge(x_split.sem, x_split.at(turn, here, ("split_x", 0, 0)))
                    if n == 0:
                        pe.wait_ge(x_kept.sem, x_kept.at(turn, here, ("keep_x", 0, 0)))
                    for side in (0, 1):
                        cols = slice(128 * f, 128 * f + rows)
                        for k, (w_half, x_half) in enumerate(((0, 0), (0, 1), (1, 0))):
                            last = nc.tensor.matmul(ps_gu[n % 2][:rows, side, :], wgu[:, w_half, m, side, cols], x16[n < HANDOVER][:, x_half, :],
                                                    start=(k == 0), stop=(k == 2))
                    last.then_inc(gu_full.sem, 1)
                elif kind == "down":
                    m, f = unit_of(n)
                    rows = F_ROWS[f]
                    pe.wait_ge(lo_done.sem, lo_done.at(turn, here, ("low", 0, n)))
                    if f == 0:
                        pe.wait_ge(y_read.sem, y_read.at(turn, here, ("y_read", 0, (n - 1) % UNITS)))
                    for t in range(QT):
                        for k, (a_half, w_half) in enumerate(((0, 0), (0, 1), (1, 0))):
                            last = nc.tensor.matmul(ps_y[:, 128 * t:128 * t + 128], a16[:rows, n % DEPTH, a_half, 128 * t:128 * t + 128],
                                                    wd[:rows, w_half, m, f, :], start=(f == 0 and t == 0 and k == 0),
                                                    stop=(f == FT - 1 and k == 2), skip_group_check=True)
                    if f == FT - 1:
                        last.then_inc(y_full.sem, 1)
                elif kind in ("max", "exp"):
                    if kind == "max":
                        full, used, bank, src, one, other, rows = max_full, max_used, ps_max, strips1[l], 0, 1, MAX_ROW
                        if n == 0:
                            pe.wait_ge(qk_read[l].sem, qk_read[l].at(turn, here, ("strips", l, 0)))
                    else:
                        full, used, bank, src, one, other, rows = exp_full, exp_used, ps_exp, strips2[l], 1, 0, MAX_ROW + 1
                        if n == 0:
                            pe.wait_ge(max_read[l].sem, max_read[l].at(turn, here, ("maxT", l, 0)))
                    pe.wait_ge(used.sem, used.before(turn, here))
                    a, t = n // 2, n % 2
                    for g in (0, 1):
                        for j in (0, 1):
                            strip = slice(STRIP * j, STRIP * j + rows)
                            last = nc.tensor.matmul(bank[:, j, g, :], src[strip, one, 2 * a + g, 128 * t:128 * t + 128],
                                                    src[strip, other, 2 * a + g, :], start=True, stop=True)
                    last.then_inc(full.sem, 1)
                elif kind in MISC:
                    pe.wait_ge(misc_out.sem, misc_out.before(turn, here))
                    if kind == "xT":
                        pe.wait_ge(normed.sem, normed.at(turn, here, ("xn", l, 0)))
                        for t in range(QT):
                            last = nc.tensor.transpose(ps_misc[:, 128 * t:128 * t + 128], xn[l][:, t, :], ident[:, :])
                    elif kind == "qk":
                        for side in (0, 1):
                            last = nc.tensor.matmul(ps_misc[:, SEQ * side:SEQ * (side + 1)], wsq[:, 4 * l + side, :], xs[l][:, :],
                                                    start=True, stop=True)
                    elif kind in ("v", "dense"):
                        for t in range(QT):
                            last = nc.tensor.matmul(ps_misc[:, 128 * t:128 * t + 128], xs[l][:, 128 * t:128 * t + 128],
                                                    wsq[:, 4 * l + 2, :] if kind == "v" else cbs[:, :], start=True, stop=True)
                    elif kind == "router":
                        for t in range(QT):
                            last = nc.tensor.matmul(ps_misc[:, EXPERTS * t:EXPERTS * (t + 1)], xs[l][:, 128 * t:128 * t + 128], gates[:, :],
                                                    start=True, stop=True)
                    elif kind == "maxT":
                        pe.wait_ge(max_used.sem, max_used.at(turn, here, ("max", l, 7)))
                        for t in range(QT):
                            last = nc.tensor.transpose(ps_misc[0:HEADS, 128 * t:128 * t + 128], row_max[l][:, t, :], ident[:, :])
                    elif kind == "pv":
                        pe.wait_ge(exp_used.sem, exp_used.at(turn, here, ("exp", l, 2 * n + 1)))
                        for t in range(QT):
                            for c in range(4):
                                last = nc.tensor.matmul(ps_misc[32 * c:32 * c + 32, 0:SEQ], V[l][:, t, 4 * n + c, :],
                                                        prob[:, n % 2, t, c % 2, c // 2, :], start=(t == 0), stop=(t == QT - 1))
                    elif kind == "norm_ctx":
                        for t in range(QT):
                            last = nc.tensor.transpose(ps_misc[:, 128 * t:128 * t + 128], pv_sb[:, n % 2, 128 * t:128 * t + 128], ident[:, :])
                    elif kind == "ctxT":
                        for t in range(QT):
                            last = nc.tensor.transpose(ps_misc[:, 128 * t:128 * t + 128], ctx_n[l][:, t, :], ident[:, :])
                    elif kind == "out":
                        for t in range(QT):
                            last = nc.tensor.matmul(ps_misc[:, 128 * t:128 * t + 128], ctx_t[l][:, 128 * t:128 * t + 128],
                                                    wsq[:, 4 * l + 3, :], start=True, stop=True)
                    last.then_inc(misc_full.sem, 1)

            pe.wait_ge(consts_in, CONSTS)
            pe.wait_ge(bv_spread, 1)
            for l in (0, 1):
                last = nc.tensor.matmul(ps_misc[:, 128 * l:128 * l + 128], bv_cols[:, l, :], wsq[:, 4 * l + 3, :], start=True, stop=True)
            last.then_inc(bv_out, 1)
            pe.wait_ge(biases_ready, 1)
            pe.wait_ge(weights_split, 1)
            pe.wait_ge(rows_in, 64)
            run(pe, stage)


def kernel(**inputs):
    import concourse.bacc as bacc
    from concourse.bass_utils import run_bass_kernel_spmd

    a = {k: np.asarray(v) for k, v in inputs.items()}
    c = np.ascontiguousarray

    x = a["L0_attn_x"].reshape(BATCHES, QT, 128, HID).transpose(0, 2, 1, 3)
    x = np.concatenate([x, np.zeros((2,) + x.shape[1:], x.dtype)])
    w_gu = np.concatenate([a["L0_ffn_base_wgu"][None], a["L0_ffn_exp_wgu"]]).transpose(1, 0, 2).reshape(128, -1)
    w_d = np.concatenate([a["L0_ffn_base_wd"][None], a["L0_ffn_exp_wd"]])
    w_d = np.pad(w_d, ((0, 0), (0, FT * 128 - INTER), (0, 0))).reshape(MLPS, FT, 128, HID).transpose(2, 0, 1, 3).reshape(128, -1)
    w_sq = np.stack([a[f"L{l}_attn_W{n}"].T for l in (0, 1) for n in "qkvo"], 1)
    b_col = np.stack([a["L0_attn_bq"], a["L0_attn_bk"], a["L1_attn_bq"], a["L1_attn_bk"], a["L0_attn_bv"], a["L1_attn_bv"]], 1)
    rows = np.stack([a["L0_attn_bo"], a["L1_attn_bo"], a["L1_ffn_SCB"], a["L1_ffn_bias"]])
    b_row = np.broadcast_to(rows[None, :, None, :], (128, 4, QT, 128))
    slopes1 = -np.power(np.float32(2.0), np.linspace(-4.0, -0.3, HEADS, dtype=np.float32)).astype(np.float32)
    both = np.stack([a["L0_attn_slopes"], slopes1])
    slopes, parts = np.zeros((128, 2, HEADS // 2), np.float32), np.zeros((128, 3), np.float32)
    k_rows = np.zeros((128, HEADS // 2, SEQ), np.float16)
    for j in (0, 1):
        for r in range(3):
            slopes[STRIP * j + PARTS * r + 3] = both[:, j::2]
            parts[STRIP * j + PARTS * r + 3, r] = 1
            k_rows[STRIP * j + PARTS * r + 3] = np.arange(SEQ)
        k_rows[STRIP * j + MAX_ROW] = SIGMA
    arrays = {
        "x": c(x), "w_gu": c(w_gu), "w_down": c(w_d), "w_sq": c(w_sq), "cb": c(a["L1_ffn_CB"].T), "gate": c(a["L0_ffn_gate_w"]),
        "b_col": c(b_col), "b_row": c(b_row), "slopes": slopes, "parts": parts, "k_rows": k_rows,
        "ident_in": np.eye(128, dtype=np.float32),
        "iota_in": c(np.broadcast_to(np.arange(EXPERTS, dtype=np.float32), (128, EXPERTS))),
    }
    nc = bacc.Bacc("TRN2", target_bir_lowering=False, num_devices=1)
    aps = [nc.dram_tensor(k, v.shape, mybir.dt.from_np(v.dtype), kind="ExternalInput").ap() for k, v in arrays.items()]
    out = nc.dram_tensor("out", (TURNS + 2, 128, QT, HID), mybir.dt.float32, kind="ExternalOutput").ap()
    build(nc, *aps, out)
    r = run_bass_kernel_spmd(nc, [arrays], core_ids=[0])
    return r.results[0]["out"][2:].transpose(0, 2, 1, 3).reshape(BATCHES, SEQ, HID)
```

```python
import numpy as np
from contextlib import ExitStack

import concourse.bass as bass
from concourse import mybir

BATCHES, SEQ, HID = 32, 256, 128
HEADS = 16
HEAD_DIM = HID // HEADS
INTER = 352
EXPERTS = 8
MLPS = EXPERTS + 1
QT = SEQ // 128
FT = -(-INTER // 128)
F_ROWS = [min(128, INTER - 128 * f) for f in range(FT)]
UNITS = MLPS * FT
TURNS = BATCHES - 1
EPS = 1e-5
DEPTH = 3

X_SCALE = 16.0
W_SCALE = 64.0
A_SCALE = 16.0
QK_SCALE = 32.0
SIGMA = QK_SCALE * QK_SCALE
GU_SCALE = X_SCALE * W_SCALE
Y_SCALE = A_SCALE * W_SCALE

STRIP = 64
PARTS = 8
MAX_ROW = PARTS * (HEAD_DIM - 1) + 3
FIELDS = (128, 128, EXPERTS, EXPERTS, HEADS, 3, 6)


HANDOVER = 15


def unit_of(w):
    u = (w - HANDOVER) % UNITS
    return u // FT, u % FT


ATTENTION = {
    0: ([("stats", 0, 0)], [("pv", 1, 3)], [("norm_ctx", 1, 3)]),
    1: ([], [("ctx_n", 1, 3)], [("strips2", 1, 0)]),
    2: ([("max", 1, 0)], [("ctxT", 1, 0)], [("aggr", 0, 0), ("norm", 0, 0), ("exp", 0, 0), ("out", 1, 0)]),
    3: ([("xn", 0, 0)], [], [("exp", 0, 1)]),
    4: ([("max", 1, 1)], [("xT", 0, 0), ("split_x", 0, 0)], []),
    5: ([("pv", 0, 0)], [("max", 1, 2)], [("norm_ctx", 0, 0), ("exp", 0, 2), ("ctx_n", 0, 0)]),
    6: ([("max", 1, 3)], [("exp", 0, 3)], [("qk", 0, 0)]),
    7: ([], [("max", 1, 4), ("split_qk", 0, 0)], [("pv", 0, 1)]),
    8: ([("v", 1, 0), ("exp", 0, 4)], [], [("norm_ctx", 0, 1)]),
    9: ([("exp", 0, 5), ("ctx_n", 0, 1), ("strips", 0, 0), ("max", 1, 5), ("router", 0, 0)], [("route", 0, 0)], [("hold", 1, 0)]),
    10: ([], [("route", 0, 1), ("max", 1, 6), ("pv", 0, 2), ("e2", 0, 0)], [("route", 0, 2)]),
    11: ([("route", 0, 3), ("norm_ctx", 0, 2)], [("route", 0, 4), ("exp", 0, 6)], [("ctx_n", 0, 2)]),
    12: ([("max", 1, 7)], [("exp", 0, 7)], []),
    13: ([("maxT", 1, 0)], [], [("route", 0, 5), ("max", 0, 0), ("pv", 0, 3)]),
    14: ([("norm_ctx", 0, 3), ("route", 0, 6)], [("ctx_n", 0, 3)], []),
    15: ([("v", 0, 0)], [("exp", 1, 0)], [("ctxT", 0, 0)]),
    16: ([("exp", 1, 1)], [("route", 0, 7)], [("max", 0, 1)]),
    17: ([("route", 0, 8)], [("pv", 1, 0)], []),
    18: ([], [("norm_ctx", 1, 0)], [("keep_x", 0, 0), ("exp", 1, 2)]),
    19: ([("ctx_n", 1, 0), ("max", 0, 2)], [("exp", 1, 3), ("out", 0, 0)], [("start", 0, 0)]),
    20: ([("stats", 1, 0)], [("aggr", 1, 0), ("load", 0, 0), ("max", 0, 3), ("strips2", 0, 0)], [("norm", 1, 0), ("pv", 1, 1)]),
    21: ([("norm_ctx", 1, 1)], [("ctx_n", 1, 1)], [("xn", 1, 0), ("max", 0, 4), ("exp", 1, 4)]),
    22: ([("xT", 1, 0), ("split_x", 1, 0)], [("exp", 1, 5)], [("max", 0, 5), ("qk", 1, 0)]),
    23: ([("max", 0, 6)], [("split_qk", 1, 0), ("pv", 1, 2)], [("exp", 1, 6)]),
    24: ([("norm_ctx", 1, 2)], [], [("ctx_n", 1, 2)]),
    25: ([("max", 0, 7)], [], []),
    26: ([("dense", 1, 0)], [], [("strips", 1, 0), ("exp", 1, 7), ("maxT", 0, 0)]),
}


def order_of_stages():
    s = []
    for w in range(UNITS):
        before = [(w - k) % UNITS for k in range(4)]
        early, middle, late = ATTENTION[w]
        if unit_of(before[3])[1] == FT - 1:
            s.append(("y_read", 0, before[3]))
        up, gate = ("up", 0, w), ("gate_u", 0, before[1])
        s += [up, gate] if w else [gate, up]
        s += [("tanh", 0, w)] + early + [("gate_g", 0, w), ("high", 0, before[1]), ("low", 0, before[1])]
        s += middle + [("down", 0, before[2])] + late
    return s


STAGES = order_of_stages()
PIPE = ("up", "high", "tanh", "gate_g", "gate_u", "low", "down", "y_read")


def ahead_of_turns():
    keep, window = [], 0
    for s in STAGES:
        kind, l, n = s
        if kind == "up":
            window = n
        if kind in PIPE:
            if n >= HANDOVER and window >= HANDOVER:
                keep.append(s)
        elif kind == "max" and l == 0:
            keep.append(s)
        elif l == 0 and kind in ("maxT", "stats", "aggr", "norm", "xn", "xT", "qk", "split_qk", "router", "route", "e2",
                                 "strips", "strips2", "v", "start", "load", "split_x", "keep_x"):
            keep.append(s)
    return keep


SPLIT_AHEAD_OF = (None, 15, 16, 18, 19, 21, UNITS, UNITS, UNITS)
SETUP_BEHIND = {("norm", 0, 0): [("biases", 0, 0)], ("qk", 0, 0): [("slopes", 0, 0), ("slopes", 1, 0)],
                ("router", 0, 0): [("weights", 0, 0)]}


def with_setup(program):
    s, held = [], []
    for stage in program:
        kind, _, n = stage
        if kind == "up":
            s += [("weights", 0, m) for m in range(1, MLPS) if SPLIT_AHEAD_OF[m] == n]
        if kind == "max":
            held.append(stage)
            s += [held.pop(0)] if len(held) > 2 else []
        else:
            s += held if kind == "maxT" else []
            s += [stage] + SETUP_BEHIND.get(stage, [])
    return s + [("weights", 0, m) for m in range(1, MLPS) if SPLIT_AHEAD_OF[m] == UNITS]


AHEAD = ahead_of_turns()
FIRST = with_setup(AHEAD)


def pass_2_alone(l):
    s = []
    for n in range(8):
        s.append(("exp", l, n))
        if n >= 2:
            s += [("pv", l, n // 2 - 1)] if n % 2 == 0 else [("norm_ctx", l, n // 2 - 1), ("ctx_n", l, n // 2 - 1)]
    return s + [("pv", l, 3), ("norm_ctx", l, 3), ("ctx_n", l, 3), ("ctxT", l, 0), ("out", l, 0)]


def merged(one, two):
    s, one, two = [], list(one), list(two)
    while one or two:
        s += [one.pop(0)] if one else []
        s += [two.pop(0)] if two else []
        s += [two.pop(0)] if s[-1][0] == "norm_ctx" else []
    return s


BESIDE_FINAL = 17


def last_turn():
    turn, pass_2 = [s for s in STAGES if s not in AHEAD], pass_2_alone(1)
    begin = turn.index(("exp", 1, 0))
    prepare = [s for s in turn[begin:] if s not in pass_2]
    maxima = [("max", 1, n) for n in range(8)]
    return (turn[:begin] + merged(prepare, pass_2[:BESIDE_FINAL]),
            merged(maxima, pass_2[BESIDE_FINAL:])
            + [("hold", 1, 0), ("v", 1, 0), ("strips2", 1, 0), ("maxT", 1, 0)])


FINAL, LAST = last_turn()
END = pass_2_alone(1)
PROGRAMS = {"first": FIRST, "turn": STAGES, "final": FINAL, "last": LAST, "end": END}
MISC = ("xT", "qk", "v", "router", "maxT", "pv", "norm_ctx", "ctxT", "out", "dense")
RANK = {name: {s: n for n, s in enumerate(p)} for name, p in PROGRAMS.items()}
LINKS = {"stats": 1, "aggr": 1, "route": 1, "norm_ctx": 1, "split_x": 1}


class Signal:

    def __init__(self, sem, signals):
        self.sem, self.signals = sem, signals
        self.done, total = {}, {}
        for name, program in PROGRAMS.items():
            count, self.done[name] = 0, {}
            for s in program:
                count += signals(s)
                self.done[name][s] = count
            total[name] = count
        self.per = total["turn"]
        self.prime = self.per - total["first"]
        self.stages = sum(signals(s) > 0 for s in STAGES)
        self.start, self.total = {"first": self.prime, "turn": self.per * TURNS}, self.per * (TURNS + 1)
        for name in ("final", "last", "end"):
            self.start[name] = self.total
            self.total += total[name]

    def before(self, turn, here):
        return self.at(turn, here, here, self.signals(here))

    def at(self, turn, here, stage, short=0):
        if not isinstance(turn, str):
            this = RANK["turn"][stage] <= RANK["turn"][here]
            return (turn + (1 if this else 0)) * self.per + (self.done["turn"][stage] - short)
        if RANK[turn].get(stage, len(STAGES)) <= RANK[turn][here]:
            return self.start[turn] + self.done[turn][stage] - short
        earlier = list(PROGRAMS)[:list(PROGRAMS).index(turn)]
        for name in reversed(earlier):
            if stage in RANK[name]:
                return self.start[name] + self.done[name][stage] - short
        return self.prime


def turn_is_first(turn):
    return isinstance(turn, str) and turn == "first"


def of(*kinds, layer=None, number=1):
    return lambda s: number if s[0] in kinds and layer in (None, s[1]) else 0


def build(nc, x, w_mlp, w_sq, fields, b_row, k_rows, out):
    f32, f16, u32 = mybir.dt.float32, mybir.dt.float16, mybir.dt.uint32
    ALU, ACT, AX = mybir.AluOpType, mybir.ActivationFunctionType, mybir.AxisListType
    with ExitStack() as ctx:
        def sb(name, shape, dt=f32):
            return ctx.enter_context(nc.sbuf_tensor(name, shape, dt))

        def sem(name):
            return ctx.enter_context(nc.semaphore(name))

        w32 = sb("w32", [128, MLPS, 2 * INTER + FT * 128])
        wgu = sb("wgu", [128, 2, MLPS, 2, INTER], f16)
        wd = sb("wd", [128, 2, MLPS, FT, 128], f16)
        wsq = sb("wsq", [128, 8, 128])
        small = sb("small", [128, sum(FIELDS)])
        starts = [sum(FIELDS[:n]) for n in range(len(FIELDS))]
        ident, cbs, gates, iota, slope_cols, part_mask, bcol = (small[:, s:s + n] for s, n in zip(starts, FIELDS))
        slope32 = slope_cols.rearrange("p (l h) -> p l h", l=2)
        bcols = sb("bcols", [128, 4])
        brow = sb("brow", [128, 4, 128])
        bv_cols = sb("bv_cols", [128, 2, 128])
        slope_rest, slope_row = sb("slope_rest", [128, 2, HEADS // 2]), sb("slope_row", [128, 2, HEADS // 2])
        slope_part = sb("slope_part", [128, 3, 2, HEADS // 2], f16)
        x_in = sb("x_in", [128, QT, HID])
        acc = sb("acc", [128, QT, HID])
        x_mid = sb("x_mid", [128, QT, HID])
        res1 = sb("res1", [128, QT, HID])
        res_hold = sb("res_hold", [128, QT, HID])
        y_out = sb("y_out", [128, QT, HID])
        x16 = [sb("x16_late", [128, 2, SEQ], f16), sb("x16_early", [128, 2, SEQ], f16)]
        xn16_1 = sb("xn16_1", [128, 2, SEQ], f16)
        xn16 = [x16[0], xn16_1]
        both = lambda name, shape, dt=f32: [sb(f"{name}{l}", shape, dt) for l in (0, 1)]
        stats, mv, rstd = both("stats", [128, QT, 6]), both("mv", [128, QT, 2]), both("rstd", [128, QT])
        var = both("var", [128, QT])
        minus_half = sb("minus_half", [128, QT])
        xn, xs = both("xn", [128, QT, HID]), both("xs", [128, SEQ])
        qk32, qk16 = both("qk32", [128, 2, SEQ]), both("qk16", [128, 2, 2, SEQ], f16)
        strips1, strips2 = both("strips1_", [128, 2, HEADS // 2, SEQ], f16), both("strips2_", [128, 2, HEADS // 2, SEQ], f16)
        V = both("V", [128, QT, HEADS, 32])
        row_max, max_t = both("row_max", [128, QT, HEADS]), both("max_t", [HEADS, SEQ], f16)
        ctx_n, ctx_t = both("ctx_n", [128, QT, HID]), both("ctx_t", [128, SEQ])
        prob = sb("prob", [128, 2, QT, 2, 2, SEQ])
        pv_sb = sb("pv_sb", [128, 2, SEQ])
        rden = sb("rden", [128, 2, QT, 4])
        tanh_sb, gated = sb("tanh_sb", [128, FT, SEQ]), sb("gated", [128, FT, SEQ])
        a32 = sb("a32", [128, DEPTH, SEQ])
        a16 = sb("a16", [128, DEPTH, 2, SEQ], f16)
        y_sb = sb("y_sb", [128, QT, HID])
        logit = sb("logit", [128, QT, EXPERTS])
        top = sb("top", [128, QT, 8])
        topi = sb("topi", [128, QT, 8], u32)
        topf = sb("topf", [128, QT, 2])
        gap, e2, den = sb("gap", [128, QT]), sb("e2", [128, QT]), sb("den", [128, QT])
        w12 = sb("w12", [128, QT, 2])
        pick = sb("pick", [128, 2, QT, EXPERTS])
        wqkv, w_dense = sb("wqkv", [128, 2, 2, 3, 128], f16), sb("w_dense", [128, 2, 128], f16)
        cw_next, cw = sb("cw_next", [128, QT, EXPERTS]), sb("cw", [128, QT, EXPERTS])

        ps_max = ctx.enter_context(nc.psum_tensor("ps_max", [128, 2, 2, SEQ], f32))
        ps_exp = ctx.enter_context(nc.psum_tensor("ps_exp", [128, 2, 2, SEQ], f32))
        ps_gu = [ctx.enter_context(nc.psum_tensor(f"ps_gu{n}", [128, 2, SEQ], f32)) for n in (0, 1)]
        ps_y = ctx.enter_context(nc.psum_tensor("ps_y", [128, 512], f32))
        ps_misc = ctx.enter_context(nc.psum_tensor("ps_misc", [128, 512], f32))

        scratch = [nc.dram_tensor(f"scratch{l}", [2, 2, 128, SEQ], f16, kind="Internal").ap() for l in (0, 1)]

        small_in, consts_in, x_first, cleared, rows_in = sem("small_in"), sem("consts_in"), sem("x_first"), sem("cleared"), sem("rows_in")
        weights_in = [sem(f"weights_in{m}") for m in range(MLPS)]
        slopes_ready, slopes_spread = sem("slopes_ready"), sem("slopes_spread")
        bv_spread, bv_out, biases_ready = sem("bv_spread"), sem("bv_out"), sem("biases_ready")
        weights_high, weights_split = sem("weights_high"), sem("weights_split")

        by_stage = []

        def signal(name, *kinds, layer=None, number=1):
            by_stage.append(Signal(sem(name), of(*kinds, layer=layer, number=number)))
            return by_stage[-1]

        misc_full = signal("misc_full", *MISC)
        misc_out = signal("misc_out", "ctx_n", *(k for k in MISC if k != "norm_ctx"))
        max_full = signal("max_full", "max", number=2)
        max_used = signal("max_used", "max", number=2)
        exp_full = signal("exp_full", "exp", number=2)
        exp_used = signal("exp_used", "exp", number=2)
        gu_full = signal("gu_full", "up")
        tanh_done = signal("tanh_done", "tanh")
        gated_done = signal("gated_done", "gate_g")
        a_done = signal("a_done", "gate_u")
        hi_done = signal("hi_done", "high")
        lo_done = signal("lo_done", "low")
        y_full = Signal(sem("y_full"), lambda s: int(s[0] == "down" and unit_of(s[2])[1] == FT - 1))
        by_stage.append(y_full)
        y_read = signal("y_read", "y_read")
        y_added = signal("y_added", "y_read")
        acc_set = signal("acc_set", "start")
        cw_set = signal("cw_set", "start")
        x_loaded = signal("x_loaded", "load", number=16)
        var_done = signal("var_done", "norm")
        rstd_done = signal("rstd_done", "norm")
        res_set = signal("res_set", "norm", layer=1)
        held = signal("held", "hold")
        normed = signal("normed", "xn")
        x_split = [signal(f"x_split{l}", "split_x", layer=l) for l in (0, 1)]
        x_kept = signal("x_kept", "keep_x")
        qk_high = signal("qk_high", "split_qk")
        qk_low = signal("qk_low", "split_qk")
        qk_written = signal("qk_written", "split_qk", number=16)
        qk_read = [signal(f"qk_read{l}", "strips", layer=l, number=96) for l in (0, 1)]
        copied = [signal(f"copied{l}", "strips2", layer=l, number=16) for l in (0, 1)]
        max_read = [signal(f"max_read{l}", "maxT", layer=l, number=32) for l in (0, 1)]
        gap_ready = Signal(sem("gap_ready"), lambda s: int(s == ("route", 0, 1)))
        by_stage.append(gap_ready)
        e2_ready = signal("e2_ready", "e2")
        stored = signal("stored", "out", layer=1, number=16)
        dve_link = Signal(sem("dve_link"), lambda s: LINKS.get(s[0], 0))
        by_stage.append(dve_link)
        CONSTS = 16 * 2

        def run(engine, stage):
            for s in FIRST:
                stage(*s, "first")
            engine.wait_ge(weights_split, MLPS)
            for g in by_stage:
                if g.stages > 1:
                    engine.wait_ge(g.sem, g.per)
            with engine.Fori(0, TURNS) as i:
                for s in STAGES:
                    stage(*s, i)
            for name in ("final", "last", "end"):
                for s in PROGRAMS[name]:
                    stage(*s, name)

        block = ctx.enter_context(nc.Block())

        @block.sync
        def _(sp):
            sp.dma_start(small[:, :], fields).then_inc(small_in, 16)
            sp.dma_start(x_in[:, :, :], x[0]).then_inc(x_first, 16)
            sp.dma_start(brow[:, :, :], b_row).then_inc(consts_in, 16)
            sp.dma_start(wsq[:, :, :], w_sq).then_inc(consts_in, 16)
            for m in (0, 1):
                sp.dma_start(w32[:, m, :], w_mlp[:, m, :]).then_inc(weights_in[m], 16)
            for g in by_stage:
                if g.prime:
                    sp.sem_inc(g.sem, g.prime)
            for l in (0, 1):
                for strips in (strips1[l], strips2[l]):
                    sp.dma_start(strips[:, 1, :, :], k_rows).then_inc(rows_in, 16)
            for m in range(2, MLPS):
                sp.dma_start(w32[:, m, :], w_mlp[:, m, :]).then_inc(weights_in[m], 16)

            def number(value):
                return value if isinstance(value, int) else sp.to_reg(value)

            def wait_first(signal, turn, here, stage):
                value = signal.at(turn, here, stage)
                if not isinstance(value, int):
                    value = sp.to_reg(value)
                    sp.wait_ge(cleared, 1)
                sp.wait_ge(signal.sem, value)

            def stage(kind, l, n, turn):
                here = (kind, l, n)
                if kind == "load":
                    wait_first(acc_set, turn, here, ("start", 0, 0))
                    batch = 1 if isinstance(turn, str) else turn + 2
                    sp.dma_start(x_in[:, :, :], x[batch]).then_inc(x_loaded.sem, 16)
                elif kind == "split_qk":
                    sp.wait_ge(qk_low.sem, qk_low.at(turn, here, here))
                    sp.dma_start(scratch[l].rearrange("a s p t -> p a s t"), qk16[l][:, :, :, :]).then_inc(qk_written.sem, 16)
                elif kind == "strips":
                    through = number(max_full.at(turn, here, ("max", l, 7)))
                    written, kept = number(qk_written.at(turn, here, ("split_qk", l, 0))), number(copied[l].at(turn, here, ("strips2", l, 0)))
                    sp.wait_ge(max_full.sem, through)
                    sp.wait_ge(copied[l].sem, kept)
                    sp.wait_ge(qk_written.sem, written)
                    for side, halves in ((0, (0, 0, 1)), (1, (0, 1, 0))):
                        for r, half in enumerate(halves):
                            sp.dma_start(strips1[l][r:128:PARTS, side, :, :],
                                         scratch[l][half, side].rearrange("(g p) t -> p g t", p=16)).then_inc(qk_read[l].sem, 16)
                elif kind == "strips2":
                    through, there = number(exp_full.at(turn, here, ("exp", l, 7))), number(qk_read[l].at(turn, here, ("strips", l, 0)))
                    sp.wait_ge(exp_full.sem, through)
                    sp.wait_ge(qk_read[l].sem, there)
                    sp.dma_start(strips2[l][:, :, :, :], strips1[l][:, :, :, :]).then_inc(copied[l].sem, 16)
                elif kind == "maxT":
                    there, copy = number(misc_out.at(turn, here, here)), number(copied[l].at(turn, here, ("strips2", l, 0)))
                    sp.wait_ge(misc_out.sem, there)
                    sp.wait_ge(copied[l].sem, copy)
                    for j in (0, 1):
                        row = STRIP * j + MAX_ROW
                        sp.dma_start(strips2[l][row:row + 1, 0, :, :], max_t[l][j:HEADS:2, :]).then_inc(max_read[l].sem, 16)
                elif kind == "out" and l == 1:
                    wait_first(misc_out, turn, here, here)
                    batch = {"final": TURNS, "last": TURNS + 1, "end": TURNS + 2}[turn] if isinstance(turn, str) else turn
                    sp.dma_start(out[batch], y_out[:, :, :]).then_inc(stored.sem, 16)

            run(sp, stage)
            sp.wait_ge(stored.sem, stored.total)
            sp.wait_ge(qk_written.sem, qk_written.total)

        @block.gpsimd
        def _(pool):
            nc.gpsimd.memset(minus_half[:, :], -0.5).then_inc(cleared, 1)
            pool.wait_ge(cleared, 1)
            nc.gpsimd.memset(prob[:, :, :, :, :, :], 1.0).then_inc(cleared, 1)

            def stage(kind, l, n, turn):
                here = (kind, l, n)
                if kind == "biases":
                    pool.wait_ge(biases_ready, 1)
                    pool.wait_ge(x_first, 16)
                elif kind == "low":
                    rows, b = F_ROWS[unit_of(n)[1]], n % DEPTH
                    pool.wait_ge(hi_done.sem, hi_done.at(turn, here, ("high", 0, n)))
                    nc.gpsimd.tensor_tensor(a16[:rows, b, 1, :], a32[:rows, b, :], a16[:rows, b, 0, :],
                                            ALU.subtract).then_inc(lo_done.sem, 1)
                elif kind == "norm":
                    pool.wait_ge(var_done.sem, var_done.at(turn, here, here))
                    nc.gpsimd.tensor_tensor(rstd[l][:, :], var[l][:, :], minus_half[:, :], ALU.pow).then_inc(rstd_done.sem, 1)
                    if l:
                        pool.wait_ge(held.sem, held.at(turn, here, ("hold", 1, 0)))
                        nc.gpsimd.tensor_tensor(res1[:, :, :], x_mid[:, :, :], brow[:, 1:2, :].to_broadcast([128, QT, HID]), ALU.add).then_inc(res_set.sem, 1)
                elif kind == "split_qk":
                    pool.wait_ge(qk_high.sem, qk_high.at(turn, here, here))
                    nc.gpsimd.tensor_tensor(qk16[l][:, 1], qk32[l][:, :, :], qk16[l][:, 0], ALU.subtract).then_inc(qk_low.sem, 1)
                elif kind == "start":
                    pool.wait_ge(misc_out.sem, misc_out.at(turn, here, ("out", 0, 0)))
                    if not isinstance(turn, str):
                        pool.wait_ge(x_loaded.sem, x_loaded.at(turn, here, ("load", 0, 0)))
                    nc.gpsimd.tensor_tensor(acc[:, :, :], x_in[:, :, :], brow[:, 0:1, :].to_broadcast([128, QT, HID]), ALU.add).then_inc(acc_set.sem, 1)
                elif kind == "y_read":
                    pool.wait_ge(y_read.sem, y_read.at(turn, here, here))
                    pool.wait_ge(acc_set.sem, acc_set.at(turn, here, ("start", 0, 0)))
                    pool.wait_ge(y_added.sem, y_added.before(turn, here))
                    nc.gpsimd.tensor_tensor(acc[:, :, :], acc[:, :, :], y_sb[:, :, :], ALU.add).then_inc(y_added.sem, 1)

            run(pool, stage)

        @block.scalar
        def _(act):
            def stage(kind, l, n, turn):
                here = (kind, l, n)
                if kind == "biases":
                    act.wait_ge(cleared, 2)
                    act.wait_ge(biases_ready, 1)
                elif kind == "high":
                    rows, b = F_ROWS[unit_of(n)[1]], n % DEPTH
                    act.wait_ge(a_done.sem, a_done.at(turn, here, ("gate_u", 0, n)))
                    nc.scalar.activation(a16[:rows, b, 0, :], a32[:rows, b, :], ACT.Copy).then_inc(hi_done.sem, 1)
                elif kind == "weights":
                    act.wait_ge(weights_in[n], 16)
                    nc.scalar.activation(wgu[:, 0, n].rearrange("p s f -> p (s f)"), w32[:, n, 0:2 * INTER], ACT.Copy, scale=W_SCALE)
                    nc.scalar.activation(wd[:, 0, n].rearrange("p f n -> p (f n)"), w32[:, n, 2 * INTER:], ACT.Copy,
                                         scale=W_SCALE).then_inc(weights_high, 1)
                elif kind == "tanh":
                    rows = F_ROWS[unit_of(n)[1]]
                    act.wait_ge(gu_full.sem, gu_full.at(turn, here, ("up", 0, n)))
                    nc.scalar.activation(tanh_sb[:rows, n % FT, :], ps_gu[n % 2][:rows, 0, :], ACT.Tanh,
                                         scale=0.5 / GU_SCALE).then_inc(tanh_done.sem, 1)
                elif kind == "y_read":
                    m = unit_of(n)[0]
                    act.wait_ge(y_full.sem, y_full.at(turn, here, ("down", 0, n)))
                    act.wait_ge(y_added.sem, y_added.before(turn, here))
                    if m:
                        act.wait_ge(cw_set.sem, cw_set.at(turn, here, ("start", 0, 0)))
                    for t in range(QT):
                        by = cw[:, t, m - 1:m] if m else 1.0 / Y_SCALE
                        last = nc.scalar.activation(y_sb[:, t, :], ps_y[:, 128 * t:128 * t + 128], ACT.Copy, scale=by)
                    last.then_inc(y_read.sem, 1)
                elif kind == "exp":
                    for j in (0, 1):
                        act.wait_ge(exp_full.sem, exp_full.at(turn, here, here, 1 - j))
                        nc.scalar.activation(prob[:, n // 2 % 2, n % 2, j], ps_exp[:, j], ACT.Exp, scale=1.0 / SIGMA).then_inc(exp_used.sem, 1)
                elif kind in ("xT", "qk", "v", "maxT", "pv", "ctxT"):
                    act.wait_ge(misc_full.sem, misc_full.at(turn, here, here))
                    if kind == "xT":
                        last = nc.scalar.activation(xs[l][:, :], ps_misc[:, 0:SEQ], ACT.Copy, scale=X_SCALE)
                    elif kind == "qk":
                        nc.scalar.activation(qk32[l][:, 0, :], ps_misc[:, 0:SEQ], ACT.Identity, bias=bcols[:, 2 * l:2 * l + 1],
                                             scale=QK_SCALE / GU_SCALE / float(np.sqrt(HEAD_DIM)))
                        last = nc.scalar.activation(qk32[l][:, 1, :], ps_misc[:, SEQ:2 * SEQ], ACT.Identity,
                                                    bias=bcols[:, 2 * l + 1:2 * l + 2], scale=QK_SCALE / GU_SCALE)
                    elif kind == "v":
                        last = nc.scalar.activation(V[l][:, :, :, 0:HEAD_DIM],
                                                    ps_misc[:, 0:QT * HID].rearrange("p (t h d) -> p t h d", t=QT, d=HEAD_DIM),
                                                    ACT.Copy, scale=1.0 / GU_SCALE)
                    elif kind == "maxT":
                        last = nc.scalar.activation(max_t[l][:, :], ps_misc[0:HEADS, 0:SEQ], ACT.Copy, scale=-1.0 / SIGMA)
                    elif kind == "pv":
                        last = nc.scalar.activation(pv_sb[:, n % 2, :], ps_misc[:, 0:SEQ], ACT.Copy)
                    else:
                        last = nc.scalar.activation(ctx_t[l][:, :], ps_misc[:, 0:SEQ], ACT.Copy)
                    last.then_inc(misc_out.sem, 1)
                elif kind == "e2":
                    act.wait_ge(gap_ready.sem, gap_ready.at(turn, here, ("route", 0, 1)))
                    nc.scalar.activation(e2[:, :], gap[:, :], ACT.Exp).then_inc(e2_ready.sem, 1)

            run(act, stage)

        @block.vector
        def _(dve):
            def number(value):
                return value if isinstance(value, int) else dve.to_reg(value)

            chain = sem("setup_chain")
            done = [0]

            def then(ins):
                done[0] += 1
                ins.then_inc(chain, 1)
                dve.wait_ge(chain, done[0])

            def stage(kind, l, n, turn):
                here = (kind, l, n)

                def linked(stage, plain=False):
                    value = number(dve_link.at(turn, here, stage))
                    if plain:
                        dve.wait_ge(small_in, 16)
                    dve.wait_ge(dve_link.sem, value)

                if kind == "biases":
                    dve.wait_ge(consts_in, CONSTS)
                    for l in (0, 1):
                        nc.vector.tensor_scalar(bcols[:, 2 * l:2 * l + 1], bcol[:, 2 * l:2 * l + 1], QK_SCALE / float(np.sqrt(HEAD_DIM)), None, ALU.mult)
                        nc.vector.tensor_scalar(bcols[:, 2 * l + 1:2 * l + 2], bcol[:, 2 * l + 1:2 * l + 2], QK_SCALE, None, ALU.mult)
                    then(nc.vector.tensor_tensor(brow[:, 1], brow[:, 1], brow[:, 3], ALU.add))
                    then(nc.vector.tensor_scalar(brow[:, 2, :], brow[:, 2, :], 1.0 / 127.0, None, ALU.mult))
                    then(nc.vector.tensor_tensor(cbs[:, :], cbs[:, :], brow[:, 2, :], ALU.mult))
                    dve.wait_ge(bv_out, 1)
                    for l in (0, 1):
                        last = nc.vector.tensor_tensor(brow[:, l, :], ps_misc[:, 128 * l:128 * l + 128], brow[:, l, :], ALU.add)
                    last.then_inc(biases_ready, 1)
                    square = wsq[:, :, :].rearrange("p (l s) n -> p l s n", l=2)[:, :, 0:3, :]
                    for split, src in ((wqkv, square), (w_dense, cbs)):
                        then(nc.vector.tensor_scalar(split[:, 0], src, W_SCALE, None, ALU.mult))
                        nc.vector.scalar_tensor_tensor(split[:, 1], src, W_SCALE, split[:, 0], op0=ALU.mult, op1=ALU.subtract)
                elif kind == "weights":
                    dve.wait_ge(weights_in[n], 16)
                    dve.wait_ge(weights_high, n + 1)
                    for lo, hi, src in ((wgu[:, 1, n].rearrange("p s f -> p (s f)"), wgu[:, 0, n].rearrange("p s f -> p (s f)"), w32[:, n, 0:2 * INTER]),
                                        (wd[:, 1, n].rearrange("p f n -> p (f n)"), wd[:, 0, n].rearrange("p f n -> p (f n)"), w32[:, n, 2 * INTER:])):
                        last = nc.vector.scalar_tensor_tensor(lo, src, W_SCALE, hi, op0=ALU.mult, op1=ALU.subtract)
                    last.then_inc(weights_split, 1)
                elif kind == "slopes":
                    dve.wait_ge(slopes_ready, 1)
                    for strips in (strips1[l], strips2[l]):
                        last = nc.vector.tensor_copy(strips[:, 0, :, :], slope_row[:, l, :].unsqueeze(2).to_broadcast([128, HEADS // 2, SEQ]))
                    last.then_inc(slopes_spread, 1)
                elif kind == "start":
                    dve.wait_ge(y_read.sem, y_read.at(turn, here, ("y_read", 0, HANDOVER - 1)))
                    linked(("route", 0, 8))
                    nc.vector.tensor_copy(cw[:, :, :], cw_next[:, :, :]).then_inc(cw_set.sem, 1)
                elif kind == "stats":
                    src = x_mid if l else x_in
                    if l:
                        dve.wait_ge(misc_out.sem, misc_out.at(turn, here, ("out", 0, 0)))
                    elif isinstance(turn, str):
                        dve.wait_ge(x_first, 16)
                    else:
                        dve.wait_ge(x_loaded.sem, x_loaded.at(turn, here, ("load", 0, 0)))
                    for t in range(QT):
                        last = nc.vector.bn_stats(stats[l][:, t, :], src[:, t, :])
                    last.then_inc(dve_link.sem, 1)
                elif kind == "aggr":
                    linked(("stats", l, 0), plain=True)
                    for t in range(QT):
                        last = nc.vector.bn_aggr(mv[l][:, t, :], stats[l][:, t, :])
                    last.then_inc(dve_link.sem, 1)
                elif kind == "norm":
                    linked(("aggr", l, 0))
                    nc.vector.tensor_scalar(var[l][:, :], mv[l][:, :, 1], EPS, None, ALU.add).then_inc(var_done.sem, 1)
                elif kind == "xn":
                    src = x_mid if l else x_in
                    dve.wait_ge(rstd_done.sem, rstd_done.at(turn, here, ("norm", l, 0)))
                    for t in range(QT):
                        last = nc.vector.tensor_scalar(xn[l][:, t, :], src[:, t, :], mv[l][:, t, 0:1], rstd[l][:, t:t + 1],
                                                       ALU.subtract, ALU.mult)
                    last.then_inc(normed.sem, 1)
                elif kind == "max":
                    a, t = n // 2, n % 2
                    dst = row_max[l][:, t, 4 * a:4 * a + 4].rearrange("p (g j) -> p j g", j=2)
                    for j in (0, 1):
                        dve.wait_ge(max_full.sem, max_full.at(turn, here, here, 1 - j))
                        nc.vector.tensor_reduce(dst[:, j], ps_max[:, j], axis=AX.X, op=ALU.max).then_inc(max_used.sem, 1)
                elif kind == "gate_g":
                    rows = F_ROWS[unit_of(n)[1]]
                    dve.wait_ge(tanh_done.sem, tanh_done.at(turn, here, ("tanh", 0, n)))
                    nc.vector.scalar_tensor_tensor(gated[:rows, n % FT, :], tanh_sb[:rows, n % FT, :], 1.0,
                                                   ps_gu[n % 2][:rows, 0, :], op0=ALU.add, op1=ALU.mult).then_inc(gated_done.sem, 1)
                elif kind == "gate_u":
                    rows = F_ROWS[unit_of(n)[1]]
                    dve.wait_ge(gated_done.sem, gated_done.at(turn, here, ("gate_g", 0, n)))
                    nc.vector.scalar_tensor_tensor(a32[:rows, n % DEPTH, :], gated[:rows, n % FT, :], 0.5 * A_SCALE / GU_SCALE ** 2,
                                                   ps_gu[n % 2][:rows, 1, :], op0=ALU.mult, op1=ALU.mult).then_inc(a_done.sem, 1)
                elif kind == "split_qk":
                    dve.wait_ge(misc_out.sem, misc_out.at(turn, here, ("qk", l, 0)))
                    nc.vector.tensor_copy(qk16[l][:, 0], qk32[l][:, :, :]).then_inc(qk_high.sem, 1)
                elif kind == "split_x":
                    if l:
                        dve.wait_ge(misc_out.sem, misc_out.at(turn, here, ("v", 1, 0)))
                    else:
                        dve.wait_ge(x_kept.sem, x_kept.at(turn, here, ("keep_x", 0, 0)))
                        dve.wait_ge(gu_full.sem, gu_full.at(turn, here, ("up", 0, UNITS - 1)))
                    dve.wait_ge(misc_out.sem, misc_out.at(turn, here, ("xT", l, 0)))
                    nc.vector.tensor_copy(xn16[l][:, 0, :], xs[l][:, :]).then_inc(dve_link.sem, 1)
                    linked(here)
                    nc.vector.tensor_tensor(xn16[l][:, 1, :], xs[l][:, :], xn16[l][:, 0, :], ALU.subtract).then_inc(x_split[l].sem, 1)
                elif kind == "keep_x":
                    dve.wait_ge(gu_full.sem, gu_full.at(turn, here, ("up", 0, HANDOVER - 1)))
                    dve.wait_ge(x_split[0].sem, x_split[0].at(turn, here, ("split_x", 0, 0)))
                    nc.vector.tensor_copy(x16[1][:, :, :], x16[0][:, :, :]).then_inc(x_kept.sem, 1)
                elif kind == "router":
                    dve.wait_ge(misc_full.sem, misc_full.at(turn, here, here))
                    nc.vector.tensor_scalar(logit[:, :, :], ps_misc[:, 0:QT * EXPERTS].rearrange("p (t e) -> p t e", t=QT),
                                            1.0 / X_SCALE, None, ALU.mult).then_inc(misc_out.sem, 1)
                elif kind == "route":
                    if n:
                        linked(("route", 0, n - 1))
                    if n == 0:
                        value = number(misc_out.at(turn, here, ("router", 0, 0)))
                        dve.wait_ge(small_in, 16)
                        dve.wait_ge(misc_out.sem, value)
                        for t in range(QT):
                            last = nc.vector.max(top[:, t, :], logit[:, t, :])
                    elif n == 1:
                        nc.vector.tensor_tensor(gap[:, :], top[:, :, 1], top[:, :, 0], ALU.subtract).then_inc(gap_ready.sem, 1)
                        for t in range(QT):
                            last = nc.vector.max_index(topi[:, t, :], top[:, t, :], logit[:, t, :])
                    elif n == 2:
                        last = nc.vector.tensor_copy(topf[:, :, :], topi[:, :, 0:2])
                    elif n == 3:
                        last = nc.vector.tensor_tensor(pick[:, :, :, :], iota[:, :].unsqueeze(1).unsqueeze(1).to_broadcast([128, 2, QT, EXPERTS]),
                                                       topf[:, :, :].rearrange("p t c -> p c t").unsqueeze(3).to_broadcast([128, 2, QT, EXPERTS]),
                                                       ALU.is_equal)
                    elif n == 4:
                        dve.wait_ge(e2_ready.sem, e2_ready.at(turn, here, ("e2", 0, 0)))
                        last = nc.vector.tensor_scalar(den[:, :], e2[:, :], 1.0, Y_SCALE, ALU.add, ALU.mult)
                    elif n == 5:
                        last = nc.vector.reciprocal(w12[:, :, 0], den[:, :])
                    elif n == 6:
                        last = nc.vector.tensor_tensor(w12[:, :, 1], e2[:, :], w12[:, :, 0], ALU.mult)
                    elif n == 7:
                        last = nc.vector.tensor_tensor(pick[:, :, :, :], pick[:, :, :, :],
                                                       w12[:, :, :].rearrange("p t c -> p c t").unsqueeze(3).to_broadcast([128, 2, QT, EXPERTS]),
                                                       ALU.mult)
                    else:
                        last = nc.vector.tensor_tensor(cw_next[:, :, :], pick[:, 0], pick[:, 1], ALU.add)
                    last.then_inc(dve_link.sem, 1)
                elif kind == "norm_ctx":
                    dve.wait_ge(misc_full.sem, misc_full.at(turn, here, here))
                    src = ps_misc[:, 0:QT * 128].rearrange("p (t h d) -> p t h d", t=QT, d=32)
                    nc.vector.reciprocal(rden[:, n % 2], src[:, :, :, HEAD_DIM]).then_inc(dve_link.sem, 1)
                elif kind == "ctx_n":
                    linked(("norm_ctx", l, n))
                    src = ps_misc[:, 0:QT * 128].rearrange("p (t h d) -> p t h d", t=QT, d=32)
                    dst = ctx_n[l][:, :, 32 * n:32 * n + 32].rearrange("p t (h d) -> p t h d", d=HEAD_DIM)
                    nc.vector.tensor_tensor(dst, src[:, :, :, 0:HEAD_DIM], rden[:, n % 2].unsqueeze(3).to_broadcast([128, QT, 4, HEAD_DIM]),
                                            ALU.mult).then_inc(misc_out.sem, 1)
                elif kind == "hold":
                    dve.wait_ge(misc_out.sem, misc_out.at(turn, here, ("out", 1, 0)))
                    nc.vector.tensor_copy(res_hold[:, :, :], res1[:, :, :]).then_inc(held.sem, 1)
                elif kind in ("out", "dense"):
                    dve.wait_ge(misc_full.sem, misc_full.at(turn, here, here))
                    src = ps_misc[:, 0:QT * HID].rearrange("p (t d) -> p t d", t=QT)
                    if kind == "dense":
                        dve.wait_ge(res_set.sem, res_set.at(turn, here, ("norm", 1, 0)))
                        last = nc.vector.scalar_tensor_tensor(res1[:, :, :], src, 1.0 / GU_SCALE, res1[:, :, :], op0=ALU.mult, op1=ALU.add)
                    elif l == 0:
                        dve.wait_ge(y_added.sem, y_added.at(turn, here, ("y_read", 0, HANDOVER - 1)))
                        last = nc.vector.tensor_tensor(x_mid[:, :, :], src, acc[:, :, :], ALU.add)
                    else:
                        dve.wait_ge(held.sem, held.at(turn, here, ("hold", 1, 0)))
                        dve.wait_ge(stored.sem, stored.before(turn, here))
                        last = nc.vector.tensor_tensor(y_out[:, :, :], src, res_hold[:, :, :], ALU.add)
                    last.then_inc(misc_out.sem, 1)

            for tile in (res1[:, :, :], res_hold[:, :, :], ctx_n[1][:, :, :], xn16_1[:, :, :]):
                nc.vector.memset(tile, 0.0)
            for l in (0, 1):
                last = nc.vector.memset(V[l][:, :, :, :], 0.0)
            then(last)
            for l in (0, 1):
                last = nc.vector.memset(V[l][:, :, :, HEAD_DIM:HEAD_DIM + 1], 1.0)
            dve.wait_ge(small_in, 16)
            for l in (0, 1):
                last = nc.vector.tensor_copy(bv_cols[:, l, :], bcol[:, 4 + l:5 + l].to_broadcast([128, 128]))
            last.then_inc(bv_spread, 1)
            then(nc.vector.tensor_scalar(slope32[:, :, :], slope32[:, :, :], SIGMA, None, ALU.mult))
            then(nc.vector.tensor_copy(slope_part[:, 0], slope32[:, :, :]))
            then(nc.vector.tensor_tensor(slope_rest[:, :, :], slope32[:, :, :], slope_part[:, 0], ALU.subtract))
            then(nc.vector.tensor_copy(slope_part[:, 1], slope_rest[:, :, :]))
            then(nc.vector.tensor_tensor(slope_part[:, 2], slope_rest[:, :, :], slope_part[:, 1], ALU.subtract))
            then(nc.vector.tensor_scalar(slope_row[:, :, :], slope_part[:, 0], part_mask[:, 0:1], None, ALU.mult))
            for r in (1, 2):
                last = nc.vector.scalar_tensor_tensor(slope_row[:, :, :], slope_part[:, r], part_mask[:, r:r + 1], slope_row[:, :, :],
                                                      op0=ALU.mult, op1=ALU.add)
                if r == 1:
                    then(last)
            last.then_inc(slopes_ready, 1)
            run(dve, stage)

        @block.tensor
        def _(pe):
            def stage(kind, l, n, turn):
                here = (kind, l, n)
                if kind == "biases":
                    pe.wait_ge(biases_ready, 1)
                elif kind == "up":
                    m, f = unit_of(n)
                    rows = F_ROWS[f]
                    before = n - 2 if n >= 2 else UNITS - 1 - n
                    pe.wait_ge(a_done.sem, a_done.at(turn, here, ("gate_u", 0, before)))
                    if turn_is_first(turn):
                        pe.wait_ge(weights_split, m + 1)
                    if n == HANDOVER:
                        pe.wait_ge(x_split[0].sem, x_split[0].at(turn, here, ("split_x", 0, 0)))
                    if n == 0:
                        pe.wait_ge(x_kept.sem, x_kept.at(turn, here, ("keep_x", 0, 0)))
                    for side in (0, 1):
                        cols = slice(128 * f, 128 * f + rows)
                        for k, (w_half, x_half) in enumerate(((0, 0), (0, 1), (1, 0))):
                            last = nc.tensor.matmul(ps_gu[n % 2][:rows, side, :], wgu[:, w_half, m, side, cols], x16[n < HANDOVER][:, x_half, :],
                                                    start=(k == 0), stop=(k == 2))
                    last.then_inc(gu_full.sem, 1)
                elif kind == "down":
                    m, f = unit_of(n)
                    rows = F_ROWS[f]
                    pe.wait_ge(lo_done.sem, lo_done.at(turn, here, ("low", 0, n)))
                    if f == 0:
                        pe.wait_ge(y_read.sem, y_read.at(turn, here, ("y_read", 0, (n - 1) % UNITS)))
                    for t in range(QT):
                        for k, (a_half, w_half) in enumerate(((0, 0), (0, 1), (1, 0))):
                            last = nc.tensor.matmul(ps_y[:, 128 * t:128 * t + 128], a16[:rows, n % DEPTH, a_half, 128 * t:128 * t + 128],
                                                    wd[:rows, w_half, m, f, :], start=(f == 0 and t == 0 and k == 0),
                                                    stop=(f == FT - 1 and k == 2), skip_group_check=True)
                    if f == FT - 1:
                        last.then_inc(y_full.sem, 1)
                elif kind in ("max", "exp"):
                    if kind == "max":
                        full, used, bank, src, one, other, rows = max_full, max_used, ps_max, strips1[l], 0, 1, MAX_ROW
                        if n == 0 and turn_is_first(turn):
                            pe.wait_ge(slopes_spread, 2)
                            pe.wait_ge(rows_in, 64)
                        if n == 0:
                            pe.wait_ge(qk_read[l].sem, qk_read[l].at(turn, here, ("strips", l, 0)))
                    else:
                        full, used, bank, src, one, other, rows = exp_full, exp_used, ps_exp, strips2[l], 1, 0, MAX_ROW + 1
                        if n == 0:
                            pe.wait_ge(max_read[l].sem, max_read[l].at(turn, here, ("maxT", l, 0)))
                    a, t = n // 2, n % 2
                    for j in (0, 1):
                        pe.wait_ge(used.sem, used.before(turn, here) - (1 - j))
                        for g in (0, 1):
                            strip = slice(STRIP * j, STRIP * j + rows)
                            last = nc.tensor.matmul(bank[:, j, g, :], src[strip, one, 2 * a + g, 128 * t:128 * t + 128],
                                                    src[strip, other, 2 * a + g, :], start=True, stop=True)
                        last.then_inc(full.sem, 1)
                elif kind in MISC:
                    pe.wait_ge(misc_out.sem, misc_out.before(turn, here))
                    if kind == "xT":
                        pe.wait_ge(normed.sem, normed.at(turn, here, ("xn", l, 0)))
                        for t in range(QT):
                            last = nc.tensor.transpose(ps_misc[:, 128 * t:128 * t + 128], xn[l][:, t, :], ident[:, :])
                    elif kind == "qk":
                        pe.wait_ge(x_split[l].sem, x_split[l].at(turn, here, ("split_x", l, 0)))
                        for side in (0, 1):
                            for k, (w_half, x_half) in enumerate(((0, 0), (0, 1), (1, 0))):
                                last = nc.tensor.matmul(ps_misc[:, SEQ * side:SEQ * (side + 1)], wqkv[:, w_half, l, side, :], xn16[l][:, x_half, :],
                                                        start=(k == 0), stop=(k == 2))
                    elif kind in ("v", "dense"):
                        for t in range(QT):
                            for k, (w_half, x_half) in enumerate(((0, 0), (0, 1), (1, 0))):
                                last = nc.tensor.matmul(ps_misc[:, 128 * t:128 * t + 128], xn16[l][:, x_half, 128 * t:128 * t + 128],
                                                        wqkv[:, w_half, l, 2, :] if kind == "v" else w_dense[:, w_half, :],
                                                        start=(k == 0), stop=(k == 2))
                    elif kind == "router":
                        for t in range(QT):
                            last = nc.tensor.matmul(ps_misc[:, EXPERTS * t:EXPERTS * (t + 1)], xs[l][:, 128 * t:128 * t + 128], gates[:, :],
                                                    start=True, stop=True)
                    elif kind == "maxT":
                        pe.wait_ge(max_used.sem, max_used.at(turn, here, ("max", l, 7)))
                        for t in range(QT):
                            last = nc.tensor.transpose(ps_misc[0:HEADS, 128 * t:128 * t + 128], row_max[l][:, t, :], ident[:, :])
                    elif kind == "pv":
                        pe.wait_ge(exp_used.sem, exp_used.at(turn, here, ("exp", l, 2 * n + 1)))
                        for t in range(QT):
                            for c in range(4):
                                last = nc.tensor.matmul(ps_misc[32 * c:32 * c + 32, 0:SEQ], V[l][:, t, 4 * n + c, :],
                                                        prob[:, n % 2, t, c % 2, c // 2, :], start=(t == 0), stop=(t == QT - 1))
                    elif kind == "norm_ctx":
                        for t in range(QT):
                            last = nc.tensor.transpose(ps_misc[:, 128 * t:128 * t + 128], pv_sb[:, n % 2, 128 * t:128 * t + 128], ident[:, :])
                    elif kind == "ctxT":
                        for t in range(QT):
                            last = nc.tensor.transpose(ps_misc[:, 128 * t:128 * t + 128], ctx_n[l][:, t, :], ident[:, :])
                    elif kind == "out":
                        for t in range(QT):
                            last = nc.tensor.matmul(ps_misc[:, 128 * t:128 * t + 128], ctx_t[l][:, 128 * t:128 * t + 128],
                                                    wsq[:, 4 * l + 3, :], start=True, stop=True)
                    last.then_inc(misc_full.sem, 1)

            pe.wait_ge(small_in, 16)
            pe.wait_ge(consts_in, CONSTS)
            pe.wait_ge(bv_spread, 1)
            for l in (0, 1):
                last = nc.tensor.matmul(ps_misc[:, 128 * l:128 * l + 128], bv_cols[:, l, :], wsq[:, 4 * l + 3, :], start=True, stop=True)
            last.then_inc(bv_out, 1)
            run(pe, stage)


def kernel(**inputs):
    import concourse.bacc as bacc
    from concourse.bass_utils import run_bass_kernel_spmd

    a = {k: np.asarray(v) for k, v in inputs.items()}
    c = np.ascontiguousarray

    x = a["L0_attn_x"].reshape(BATCHES, QT, 128, HID).transpose(0, 2, 1, 3)
    x = np.concatenate([x, np.zeros((1,) + x.shape[1:], x.dtype)])
    w_gu = np.concatenate([a["L0_ffn_base_wgu"][None], a["L0_ffn_exp_wgu"]]).transpose(1, 0, 2)
    w_d = np.concatenate([a["L0_ffn_base_wd"][None], a["L0_ffn_exp_wd"]])
    w_d = np.pad(w_d, ((0, 0), (0, FT * 128 - INTER), (0, 0))).reshape(MLPS, FT, 128, HID).transpose(2, 0, 1, 3).reshape(128, MLPS, -1)
    w_sq = np.stack([a[f"L{l}_attn_W{n}"].T for l in (0, 1) for n in "qkvo"], 1)
    b_col = np.stack([a["L0_attn_bq"], a["L0_attn_bk"], a["L1_attn_bq"], a["L1_attn_bk"], a["L0_attn_bv"], a["L1_attn_bv"]], 1)
    rows = np.stack([a["L0_attn_bo"], a["L1_attn_bo"], a["L1_ffn_SCB"], a["L1_ffn_bias"]])
    b_row = np.broadcast_to(rows[None], (128, 4, 128))
    slopes1 = -np.power(np.float32(2.0), np.linspace(-4.0, -0.3, HEADS, dtype=np.float32)).astype(np.float32)
    both = np.stack([a["L0_attn_slopes"], slopes1])
    slopes, parts = np.zeros((128, 2, HEADS // 2), np.float32), np.zeros((128, 3), np.float32)
    k_rows = np.zeros((128, HEADS // 2, SEQ), np.float16)
    for j in (0, 1):
        for r in range(3):
            slopes[STRIP * j + PARTS * r + 3] = both[:, j::2]
            parts[STRIP * j + PARTS * r + 3, r] = 1
            k_rows[STRIP * j + PARTS * r + 3] = np.arange(SEQ)
        k_rows[STRIP * j + MAX_ROW] = SIGMA
    numbers = np.broadcast_to(np.arange(EXPERTS, dtype=np.float32), (128, EXPERTS))
    fields = [np.eye(128, dtype=np.float32), a["L1_ffn_CB"].T, a["L0_ffn_gate_w"], numbers, slopes.reshape(128, HEADS), parts, b_col]
    arrays = {
        "x": c(x), "w_mlp": c(np.concatenate([w_gu, w_d], 2)), "w_sq": c(w_sq), "fields": c(np.concatenate(fields, 1)),
        "b_row": c(b_row), "k_rows": k_rows,
    }
    nc = bacc.Bacc("TRN2", target_bir_lowering=False, num_devices=1)
    aps = [nc.dram_tensor(k, v.shape, mybir.dt.from_np(v.dtype), kind="ExternalInput").ap() for k, v in arrays.items()]
    out = nc.dram_tensor("out", (TURNS + 3, 128, QT, HID), mybir.dt.float32, kind="ExternalOutput").ap()
    build(nc, *aps, out)
    r = run_bass_kernel_spmd(nc, [arrays], core_ids=[0])
    return r.results[0]["out"][2:].transpose(0, 2, 1, 3).reshape(BATCHES, SEQ, HID)
```
